# Optimizing a Trainium2 kernel written in Bass

```python
import numpy as np
import jax
import jax.numpy as jnp

def _softmax(x, axis=-1):
    return jax.nn.softmax(x, axis=axis)

def _gelu(x):
    return jax.nn.gelu(x, approximate=True)

def _silu(x):
    return jax.nn.silu(x)

def _sigmoid(x):
    return jax.nn.sigmoid(x)

def _layernorm(x, axis=-1, eps=1e-05):
    m = jnp.mean(x, axis=axis, keepdims=True)
    v = jnp.var(x, axis=axis, keepdims=True)
    return (x - m) / jnp.sqrt(v + eps)

def _scatter_add(tgt, idx, src, axis=0):
    return tgt.at[idx].add(src)

def _segment_sum(src, seg, n):
    return jax.ops.segment_sum(src, seg, n)
kernel_name = 'mk_seq_preln_d1_jaxref_r8_4f601a'

def setup_inputs(seed: int=0):
    np.random.seed(seed)
    _w = jnp.asarray

    def _L0_attn_setup():
        import jax, jax.numpy as jnp
        import numpy as np
        DIM = 128
        B, T = (4, 512)
        CAP = 10.0
        EPS_N = 1e-06
        EPS_RMS = 1e-08

        def softcap(x, a=CAP):
            return a * jnp.tanh(x / a)
        key = jax.random.key(seed)
        k1, k2 = jax.random.split(key)
        x = jax.random.normal(k1, (B, T, DIM), dtype=jnp.float32)
        W = jax.random.normal(k2, (DIM, 4 * DIM), dtype=jnp.float32) / np.sqrt(DIM)
        b = jnp.zeros((4 * DIM,), dtype=jnp.float32)
        input_bias = -jnp.ones((DIM,), dtype=jnp.float32)
        scale = jnp.ones((DIM,), dtype=jnp.float32)
        return {'x': x, 'W': W, 'b': b, 'input_bias': input_bias, 'scale': scale}
    _L0_attn_in = _L0_attn_setup()

    def _L0_ffn_setup():
        import jax, jax.numpy as jnp
        import numpy as np
        B, S, D, H, E, K, F = (1, 128, 128, 16, 8, 2, 512)

        def layernorm(x, g, b, eps=1e-05):
            m = x.mean(-1, keepdims=True)
            v = ((x - m) ** 2).mean(-1, keepdims=True)
            return (x - m) * jax.lax.rsqrt(v + eps) * g + b
        key = jax.random.key(seed)
        ks = jax.random.split(key, 8)
        n = lambda k, shape, sc: jax.random.normal(k, shape, dtype=jnp.float32) * sc
        return {'x': n(ks[0], (B, S, D), 1.0), 'w_qkv': n(ks[1], (D, 3 * D), D ** (-0.5)), 'w_o': n(ks[2], (D, D), D ** (-0.5)), 'g1': jnp.ones((D,), jnp.float32), 'b1': jnp.zeros((D,), jnp.float32), 'wg': n(ks[3], (D, E), D ** (-0.5)), 'w1': n(ks[4], (E, D, F), D ** (-0.5)), 'bb1': jnp.zeros((E, F), jnp.float32), 'w2': n(ks[5], (E, F, D), F ** (-0.5)), 'bb2': jnp.zeros((E, D), jnp.float32), 'g2': jnp.ones((D,), jnp.float32), 'b2': jnp.zeros((D,), jnp.float32)}
    _L0_ffn_in = _L0_ffn_setup()
    _d = {'L0_attn_x': _L0_attn_in['x'], 'L0_attn_W': _L0_attn_in['W'], 'L0_attn_b': _L0_attn_in['b'], 'L0_attn_input_bias': _L0_attn_in['input_bias'], 'L0_attn_scale': _L0_attn_in['scale'], 'L0_ffn_w_qkv': _L0_ffn_in['w_qkv'], 'L0_ffn_w_o': _L0_ffn_in['w_o'], 'L0_ffn_g1': _L0_ffn_in['g1'], 'L0_ffn_b1': _L0_ffn_in['b1'], 'L0_ffn_wg': _L0_ffn_in['wg'], 'L0_ffn_w1': _L0_ffn_in['w1'], 'L0_ffn_bb1': _L0_ffn_in['bb1'], 'L0_ffn_w2': _L0_ffn_in['w2'], 'L0_ffn_bb2': _L0_ffn_in['bb2'], 'L0_ffn_g2': _L0_ffn_in['g2'], 'L0_ffn_b2': _L0_ffn_in['b2']}
    _x0 = _d['L0_attn_x']
    _d['L0_attn_x'] = jax.random.normal(jax.random.fold_in(jax.random.key(seed), 1), (32, 256, 128), dtype=_x0.dtype)
    del _x0
    return _d

def reference(L0_attn_x, L0_attn_W, L0_attn_b, L0_attn_input_bias, L0_attn_scale, L0_ffn_w_qkv, L0_ffn_w_o, L0_ffn_g1, L0_ffn_b1, L0_ffn_wg, L0_ffn_w1, L0_ffn_bb1, L0_ffn_w2, L0_ffn_bb2, L0_ffn_g2, L0_ffn_b2):

    def _L0_attn_ref(x, W, b, input_bias, scale):
        import jax, jax.numpy as jnp
        import numpy as np
        DIM = 128
        B, T = (4, 512)
        CAP = 10.0
        EPS_N = 1e-06
        EPS_RMS = 1e-08

        def softcap(x, a=CAP):
            return a * jnp.tanh(x / a)
        pre = jnp.einsum('btd,df->btf', x, W) + b
        i_pre, f_pre, o_pre, z = jnp.split(pre, 4, axis=-1)
        i_gate = softcap(i_pre + input_bias)
        f_gate = -jax.nn.softplus(f_pre)
        o_sig = jax.nn.sigmoid(o_pre)
        tz = jnp.tanh(z)
        seq = (jnp.swapaxes(i_gate, 0, 1), jnp.swapaxes(f_gate, 0, 1), jnp.swapaxes(o_sig, 0, 1), jnp.swapaxes(tz, 0, 1))
        c0 = jnp.zeros((x.shape[0], DIM), dtype=x.dtype)
        n0 = jnp.zeros_like(c0)
        m0 = jnp.zeros_like(c0)

        def step(carry, inp):
            c, n, m = carry
            i_t, f_t, o_t, tz_t = inp
            m_next = jnp.maximum(f_t + m, i_t)
            i_s = jnp.exp(i_t - m_next)
            f_s = jnp.exp(f_t + m - m_next)
            c = f_s * c + i_s * tz_t
            n = f_s * n + i_s
            h = o_t * (c / (n + EPS_N))
            return ((c, n, m_next), h)
        _, hs = jax.lax.scan(step, (c0, n0, m0), seq)
        out = jnp.swapaxes(hs, 0, 1)
        rms = jnp.sqrt(jnp.mean(jnp.square(out), axis=-1, keepdims=True) + EPS_RMS)
        out = out / rms * scale
        return out

    def _L0_ffn_ref(x, w_qkv, w_o, g1, b1, wg, w1, bb1, w2, bb2, g2, b2):
        import jax, jax.numpy as jnp
        import numpy as np
        B, S, D, H, E, K, F = (1, 128, 128, 16, 8, 2, 512)

        def layernorm(x, g, b, eps=1e-05):
            m = x.mean(-1, keepdims=True)
            v = ((x - m) ** 2).mean(-1, keepdims=True)
            return (x - m) * jax.lax.rsqrt(v + eps) * g + b
        b, s, d = x.shape
        hd = d // H
        qkv = x @ w_qkv
        q, k, v = jnp.split(qkv, 3, axis=-1)
        to_heads = lambda t: t.reshape(b, s, H, hd).transpose(0, 2, 1, 3)
        q, k, v = (to_heads(q), to_heads(k), to_heads(v))
        scores = jnp.einsum('bhqd,bhkd->bhqk', q, k) / jnp.sqrt(jnp.float32(hd))
        causal = jnp.tril(jnp.ones((s, s), bool))
        scores = jnp.where(causal, scores, jnp.finfo(scores.dtype).min)
        attn = jax.nn.softmax(scores, axis=-1)
        o = jnp.einsum('bhqk,bhkd->bhqd', attn, v)
        o = o.transpose(0, 2, 1, 3).reshape(b, s, d) @ w_o
        h = layernorm(x + o, g1, b1)
        probs = jax.nn.softmax(h @ wg, axis=-1)
        topv, topi = jax.lax.top_k(probs, K)
        topv = topv / topv.sum(-1, keepdims=True)
        w = (topv[..., None] * jax.nn.one_hot(topi, E, dtype=h.dtype)).sum(-2)
        h1 = jax.nn.gelu(jnp.einsum('bsd,edf->ebsf', h, w1) + bb1[:, None, None, :])
        y = jnp.einsum('ebsf,efd->ebsd', h1, w2) + bb2[:, None, None, :]
        moe = jnp.einsum('ebsd,bse->bsd', y, w)
        return layernorm(h + moe, g2, b2)
    x = L0_attn_x
    x = x + _L0_attn_ref(_layernorm(x, axis=-1), L0_attn_W, L0_attn_b, L0_attn_input_bias, L0_attn_scale)
    x = x + _L0_ffn_ref(_layernorm(x, axis=-1), L0_ffn_w_qkv, L0_ffn_w_o, L0_ffn_g1, L0_ffn_b1, L0_ffn_wg, L0_ffn_w1, L0_ffn_bb1, L0_ffn_w2, L0_ffn_bb2, L0_ffn_g2, L0_ffn_b2)
    return x

_drawn_inputs = setup_inputs


def setup_inputs(seed=0):
    import zlib

    import numpy as np

    out = dict(_drawn_inputs(seed))
    spreads = {'L0_attn_b': (0.0, 0.1),
     'L0_attn_input_bias': (-1.0, 0.6),
     'L0_attn_scale': (1.0, 0.2),
     'L0_ffn_g1': (1.0, 0.2),
     'L0_ffn_b1': (0.0, 0.1),
     'L0_ffn_bb1': (0.0, 0.427),
     'L0_ffn_bb2': (0.0, 0.301),
     'L0_ffn_g2': (1.0, 0.2),
     'L0_ffn_b2': (0.0, 0.1)}
    factors = {}
    for name, (base, spread) in spreads.items():
        noise = np.random.default_rng([zlib.crc32(name.encode()), seed]).standard_normal(out[name].shape)
        drawn = base * np.exp(spread * noise) if base else spread * noise
        out[name] = jnp.asarray(drawn.astype(out[name].dtype))
    for name, factor in factors.items():
        out[name] = (out[name] * factor).astype(out[name].dtype)
    return out
```

```python
import concourse.bass as bass
from concourse import mybir
from contextlib import ExitStack

fp32 = mybir.dt.float32
f32r = mybir.dt.float32r
bf16 = mybir.dt.bfloat16
u32 = mybir.dt.uint32
ALU = mybir.AluOpType
ACT = mybir.ActivationFunctionType
AX = mybir.AxisListType

P = 128
B, T, D = 32, 256, 128
NTILE = B * T // P
LN_EPS = 1e-5
N_EPS = 1e-6
RMS_EPS = 1e-8
CAP = 10.0
SOFTPLUS_CUT = 30.0


class Count:

    def __init__(self, base, slope=0, i=None):
        self.base, self.slope, self.i = base, slope, i

    def __add__(self, n):
        return Count(self.base + n, self.slope, self.i)

    def __sub__(self, n):
        return self + -n

    def __mul__(self, n):
        return Count(self.base * n, self.slope * n, self.i)

    __rmul__ = __mul__

    def turn(self, buffers):
        return Count(self.base // buffers, self.slope // buffers, self.i)

    def of(self, buffers):
        return self.base % buffers

    def value(self):
        return self.base if self.i is None else self.i * self.slope + self.base

    def most(self, n):
        return Count(min(self.base, n)) if self.i is None else self

    def exists(self, count):
        return self.i is not None or 0 <= self.base < count


def need(engine, sem, count):
    if count.i is None and count.base <= 0:
        return
    assert count.base > 0
    engine.wait_ge(sem, count.value())


def need_apart(engine, met, *needs):
    needs = [(sem, count) for sem, count in needs if count.i is not None or count.base > 0]
    assert all(count.base > 0 for _, count in needs)
    values = [engine.to_reg(count.value()) if count.i is not None else count.base for _, count in needs]
    engine.wait_ge(*met)
    for (sem, _), value in zip(needs, values):
        engine.wait_ge(sem, value)


def steps(engine, count, lag, unroll, step, first):
    rounds = (count - first) // unroll
    for s in range(first):
        step(Count(s))
    with engine.Fori(0, rounds) as i:
        for k in range(unroll):
            step(Count(first + k, unroll, i))
    for s in range(first + rounds * unroll, count + lag):
        step(Count(s))


def recurrent_layer(nc, dram, const):
    GROUPS = NTILE // 4
    x_t = dram["x"].rearrange("b (h p) d -> p (b h) d", p=P)
    x1_t = dram["x1"].rearrange("(t p) d -> p t d", p=P)
    ident = const["ident"]
    ctx = ExitStack()
    with ctx:
        def sb(name, shape, dt=fp32):
            return ctx.enter_context(nc.sbuf_tensor(name, shape, dt))

        def sem(name):
            return ctx.enter_context(nc.semaphore(name))

        w_f = sb("a_w_f", [P, 4 * D])
        w_hi = sb("a_w_hi", [P, 4 * D], f32r)
        w_lo = sb("a_w_lo", [P, 4 * D], f32r)
        b_col = sb("a_b_col", [P, 4])
        ib_col = sb("a_ib_col", [P, 1])
        bias_i = sb("a_bias_i", [P, 1])
        bias_o = sb("a_bias_o", [P, 1])
        scale_b = sb("a_scale_b", [P, D])
        one_col = sb("a_one", [P, 1])
        eps_ln = sb("a_eps_ln", [P, 1])
        eps_n = sb("a_eps_n", [P, 1])
        eps_rms = sb("a_eps_rms", [P, 1])
        X = sb("a_X", [P, 3, 4, D])
        stats = sb("a_stats", [P, 2, 4, 6])
        mv = sb("a_mv", [P, 2, 4, 2])
        lnv = sb("a_lnv", [P, 2, 4])
        rstd = sb("a_rstd", [P, 2, 4])
        XN = sb("a_XN", [P, 2, 4, D])
        xt_hi = sb("a_xt_hi", [P, 2, 4 * P], f32r)
        xt_lo = sb("a_xt_lo", [P, 2, 4 * P], f32r)
        f_cut = sb("a_f_cut", [P, 512])
        f_exp = sb("a_f_exp", [P, 512])
        f_ln = sb("a_f_ln", [P, 512])
        sp = sb("a_sp", [P, 2, 512])
        i_tanh = sb("a_i_tanh", [P, 2, 512])
        i_neg = sb("a_i_neg", [P, 2, 512])
        z_tanh = sb("a_z_tanh", [P, 2, 512])
        o_tanh = sb("a_o_tanh", [P, 2, 512])
        M = sb("a_M", [P, 2, 2, T + 1])
        i_arg = sb("a_i_arg", [P, 512])
        f_sum = sb("a_f_sum", [P, 512])
        f_arg = sb("a_f_arg", [P, 512])
        i_s = sb("a_i_s", [P, 512])
        f_s = sb("a_f_s", [P, 512])
        iz = sb("a_iz", [P, 512])
        C = sb("a_C", [P, 512])
        N = sb("a_N", [P, 512])
        n_ln = sb("a_n_ln", [P, 512])
        n_inv = sb("a_n_inv", [P, 512])
        oc = sb("a_oc", [P, 512])
        H2 = sb("a_H2", [P, 2, 512])
        sq = sb("a_sq", [P, D])
        ss = sb("a_ss", [P, 4])
        ln_ss = sb("a_ln_ss", [P, 4])
        r_rms = sb("a_r_rms", [P, 4])
        Y = sb("a_Y", [P, 2, 4, D])
        X1 = sb("a_X1", [P, 2, 4, D])
        ps_t = ctx.enter_context(nc.psum_tensor("a_ps_t", [P, 2, 512], fp32))
        ps_g = ctx.enter_context(nc.psum_tensor("a_ps_g", [P, 4, 512], fp32))
        ps_h = ctx.enter_context(nc.psum_tensor("a_ps_h", [P, 2, 512], fp32))
        GI, GF, GO, GZ = range(4)

        s_load = sem("a_load")
        s_prep = sem("a_prep")
        s_whi = sem("a_whi")
        s_x = [sem(f"a_x{k}") for k in range(3)]
        s_mv = sem("a_mv_s")
        s_st = sem("a_st")
        s_lnv = sem("a_lnv_s")
        s_rstd = sem("a_rstd_s")
        s_xn = sem("a_xn_s")
        s_xt = sem("a_xt_s")
        s_xhi = sem("a_xhi")
        s_xlo = sem("a_xlo")
        s_g = sem("a_g")
        s_cut = sem("a_cut")
        s_fexp = sem("a_fexp")
        s_fln = sem("a_fln")
        s_sp = sem("a_sp_s")
        s_it = sem("a_it")
        s_in = sem("a_in")
        s_zt = sem("a_zt")
        s_ot = sem("a_ot")
        s_m = sem("a_m")
        s_ia = sem("a_ia")
        s_fsum = sem("a_fsum")
        s_fa = sem("a_fa")
        s_is = sem("a_is")
        s_fs = sem("a_fs")
        s_iz = sem("a_iz_s")
        s_cn = sem("a_cn")
        s_nln = sem("a_nln")
        s_ninv = sem("a_ninv")
        s_oc = sem("a_oc_s")
        s_h2 = sem("a_h2")
        s_ht = sem("a_ht")
        s_ss = sem("a_ss_s")
        s_lnss = sem("a_lnss")
        s_rms = sem("a_rms")
        s_y = sem("a_y")
        s_x1 = sem("a_x1_s")
        s_out = [sem(f"a_out{k}") for k in range(2)]
        block = ctx.enter_context(nc.Block())

        @block.sync
        def _(sync):
            sync.dma_start(w_f[:, :], dram["W"]).then_inc(s_load, 16)
            sync.dma_start(b_col[:, :], dram["b"].rearrange("(c p) -> p c", p=P), allow_slow_non_contiguous=True).then_inc(s_load, 16)
            sync.dma_start(ib_col[:, :], dram["input_bias"].rearrange("(p a) -> p a", a=1), allow_slow_non_contiguous=True).then_inc(s_load, 16)
            sync.dma_start(scale_b[:, :], dram["scale"].partition_broadcast(P)).then_inc(s_load, 16)

            sync.wait_ge(s_load, 64)

            def step(s):
                if (s - 0).exists(GROUPS):
                    need_apart(sync, (s_load, 64), (s_x1, s - 2))
                    sync.dma_start(X[:, s.of(3)], x_t[:, bass.ds((s * 4).value(), 4), :]).then_inc(s_x[s.of(3)], 16)
                if (s - 3).exists(GROUPS):
                    g = s - 3
                    need_apart(sync, (s_load, 64), (s_x1, g + 1))
                    sync.dma_start(x1_t[:, bass.ds((g * 4).value(), 4), :], X1[:, g.of(2)]).then_inc(s_out[g.of(2)], 16)

            steps(sync, GROUPS, 3, 6, step, 6)
            for k in range(2):
                sync.wait_ge(s_out[k], 16 * GROUPS // 2)

        @block.gpsimd
        def _(pool):
            def step(s):
                if (s - 1).exists(GROUPS):
                    g = s - 1
                    j = g.of(2)
                    need(pool, s_it, g + 1)
                    need(pool, s_ia, g - 1)
                    nc.gpsimd.tensor_scalar(i_neg[:, j], i_tanh[:, j], CAP, None, ALU.mult).then_inc(s_in, 1)
                    need(pool, s_m, g + 1)
                    need(pool, s_fa, g)
                    nc.gpsimd.tensor_tensor(f_sum[:, :].rearrange("p (b t) -> p b t", b=2), M[:, j, :, 0:T],
                                            sp[:, j].rearrange("p (b t) -> p b t", b=2), ALU.add).then_inc(s_fsum, 1)
                    need(pool, s_fsum, g + 1)
                    need(pool, s_fs, g)
                    nc.gpsimd.tensor_tensor(f_arg[:, :].rearrange("p (b t) -> p b t", b=2), M[:, j, :, 1:T + 1],
                                            f_sum[:, :].rearrange("p (b t) -> p b t", b=2), ALU.subtract).then_inc(s_fa, 1)
                if (s - 2).exists(GROUPS):
                    g = s - 2
                    j = g.of(2)
                    need(pool, s_y, g + 1)
                    need(pool, s_out[j], g.turn(2) * 16)
                    nc.gpsimd.tensor_tensor(X1[:, j], Y[:, j], X[:, g.of(3)], ALU.add).then_inc(s_x1, 1)

            steps(pool, GROUPS, 2, 6, step, 6)

        @block.scalar
        def _(act):
            act.wait_ge(s_load, 64)
            act.wait_ge(s_prep, 5)
            nc.scalar.copy(w_hi[:, :], w_f[:, :]).then_inc(s_whi, 1)

            def step(s):
                j = (s - 1).of(2)
                if (s - 1).exists(GROUPS):
                    g = s - 1
                    need(act, s_g, 4 * g + 1 + GI)
                    need(act, s_in, g - 1)
                    nc.scalar.activation(i_tanh[:, j], ps_g[:, GI], ACT.Tanh, bias=bias_i[:, :], scale=-1.0 / CAP).then_inc(s_it, 1)
                    need(act, s_g, 4 * g + 1 + GO)
                    need(act, s_oc, g - 1)
                    nc.scalar.activation(o_tanh[:, j], ps_g[:, GO], ACT.Tanh, bias=bias_o[:, :], scale=0.5).then_inc(s_ot, 1)
                    need(act, s_g, 4 * g + 1 + GZ)
                    need(act, s_iz, g - 1)
                    nc.scalar.activation(z_tanh[:, j], ps_g[:, GZ], ACT.Tanh, bias=b_col[:, GZ:GZ + 1]).then_inc(s_zt, 1)
                if (s - 0).exists(GROUPS):
                    g, j0 = s, s.of(2)
                    need(act, s_mv, g + 1)
                    need(act, s_rstd, g - 1)
                    nc.scalar.activation(lnv[:, j0], mv[:, j0, :, 1], ACT.Ln, bias=eps_ln[:, :]).then_inc(s_lnv, 1)
                    need(act, s_lnv, g + 1)
                    need(act, s_xn, g - 1)
                    nc.scalar.activation(rstd[:, j0], lnv[:, j0], ACT.Exp, scale=-0.5).then_inc(s_rstd, 1)
                if (s - 1).exists(GROUPS):
                    g = s - 1
                    need(act, s_cut, g + 1)
                    need(act, s_fln, g)
                    nc.scalar.activation(f_exp[:, :], f_cut[:, :], ACT.Exp).then_inc(s_fexp, 1)
                    need(act, s_fexp, g + 1)
                    need(act, s_sp, g)
                    nc.scalar.activation(f_ln[:, :], f_exp[:, :], ACT.Ln, bias=one_col[:, :]).then_inc(s_fln, 1)
                if (s - 2).exists(GROUPS):
                    g, j0 = s - 2, s.of(2)
                    need(act, s_ht, g + 1)
                    need(act, s_lnss, g)
                    for t in range(4):
                        need(act, s_ss, 4 * g + t)
                        nc.scalar.activation(sq[:, :], ps_h[:, j0, t * P:(t + 1) * P], ACT.Square,
                                             accum_out=ss[:, t:t + 1]).then_inc(s_ss, 1)
                    need(act, s_ss, 4 * g + 4)
                    nc.scalar.activation(ln_ss[:, :], ss[:, :], ACT.Ln, bias=eps_rms[:, :], scale=1.0 / D).then_inc(s_lnss, 1)
                    need(act, s_lnss, g + 1)
                    need(act, s_y, g)
                    nc.scalar.activation(r_rms[:, :], ln_ss[:, :], ACT.Exp, scale=-0.5).then_inc(s_rms, 1)
                if (s - 0).exists(GROUPS):
                    g, j0 = s, s.of(2)
                    need(act, s_xt, g + 1)
                    need(act, s_g, 4 * (g - 1))
                    nc.scalar.copy(xt_hi[:, j0], ps_t[:, j0]).then_inc(s_xhi, 1)
                if (s - 1).exists(GROUPS):
                    g = s - 1
                    need(act, s_ia, g + 1)
                    need(act, s_cn, 2 * g)
                    nc.scalar.activation(i_s[:, :], i_arg[:, :], ACT.Exp).then_inc(s_is, 1)
                    need(act, s_fa, g + 1)
                    nc.scalar.activation(f_s[:, :], f_arg[:, :], ACT.Exp).then_inc(s_fs, 1)
                    need(act, s_cn, 2 * g + 1)
                    need(act, s_ninv, g)
                    nc.scalar.activation(n_ln[:, :], N[:, :], ACT.Ln, bias=eps_n[:, :]).then_inc(s_nln, 1)
                    need(act, s_nln, g + 1)
                    need(act, s_h2, g)
                    nc.scalar.activation(n_inv[:, :], n_ln[:, :], ACT.Exp, scale=-1.0).then_inc(s_ninv, 1)

            steps(act, GROUPS, 2, 6, step, 6)

        @block.vector
        def _(dve):
            nc.vector.memset(one_col[:, :], 1.0)
            nc.vector.memset(eps_ln[:, :], LN_EPS)
            nc.vector.memset(eps_n[:, :], N_EPS)
            nc.vector.memset(eps_rms[:, :], 4 * RMS_EPS).then_inc(s_prep, 1)
            nc.vector.memset(M[:, :, :, 0:1], 0.0).then_inc(s_prep, 1)
            dve.wait_ge(s_load, 64)
            nc.vector.tensor_tensor(bias_i[:, :], b_col[:, GI:GI + 1], ib_col[:, :], ALU.add).then_inc(s_prep, 1)
            dve.wait_ge(s_prep, 3)
            nc.vector.tensor_scalar(bias_i[:, :], bias_i[:, :], -1.0 / CAP, None, ALU.mult).then_inc(s_prep, 1)
            nc.vector.tensor_scalar(bias_o[:, :], b_col[:, GO:GO + 1], 0.5, None, ALU.mult).then_inc(s_prep, 1)
            dve.wait_ge(s_whi, 1)
            nc.vector.tensor_tensor(w_lo[:, :], w_f[:, :], w_hi[:, :].bitcast(fp32), ALU.subtract).then_inc(s_prep, 1)

            def step(s):
                j, j0 = (s - 1).of(2), s.of(2)
                if (s - 1).exists(GROUPS):
                    g = s - 1
                    need(dve, s_g, 4 * g + 1 + GF)
                    need(dve, s_fexp, g)
                    nc.vector.tensor_scalar(f_cut[:, :], ps_g[:, GF], b_col[:, GF:GF + 1], SOFTPLUS_CUT,
                                            ALU.add, ALU.min).then_inc(s_cut, 1)
                if (s - 0).exists(GROUPS):
                    g = s
                    need(dve, s_x[s.of(3)], g.turn(3) * 16 + 16)
                    for t in range(4):
                        last = nc.vector.bn_stats(stats[:, j0, t, :], X[:, s.of(3), t, :])
                    last.then_inc(s_st, 1)
                    need_apart(dve, (s_prep, 1), (s_st, g + 1), (s_lnv, g - 1))
                    for t in range(4):
                        last = nc.vector.bn_aggr(mv[:, j0, t, :], stats[:, j0, t, :])
                    last.then_inc(s_mv, 1)
                if (s - 1).exists(GROUPS):
                    g = s - 1
                    need(dve, s_fln, g + 1)
                    nc.vector.scalar_tensor_tensor(out=sp[:, j], in0=ps_g[:, GF], scalar=b_col[:, GF:GF + 1],
                                                   in1=f_ln[:, :], op0=ALU.add, op1=ALU.max).then_inc(s_sp, 1)
                    need(dve, s_sp, g + 1)
                    need(dve, s_in, g + 1)
                    for b in range(2):
                        last = nc.vector.tensor_tensor_scan(M[:, j, b, 1:T + 1], sp[:, j, b * T:(b + 1) * T],
                                                            i_neg[:, j, b * T:(b + 1) * T], 0.0, ALU.add, ALU.min)
                    last.then_inc(s_m, 1)
                    need(dve, s_m, g + 1)
                    need(dve, s_is, g)
                    nc.vector.tensor_tensor(i_arg[:, :].rearrange("p (b t) -> p b t", b=2), M[:, j, :, 1:T + 1],
                                            i_neg[:, j].rearrange("p (b t) -> p b t", b=2), ALU.subtract).then_inc(s_ia, 1)
                if (s - 0).exists(GROUPS):
                    g = s
                    need(dve, s_rstd, g + 1)
                    need(dve, s_xt, g - 1)
                    for t in range(4):
                        last = nc.vector.tensor_scalar(XN[:, j0, t, :], X[:, s.of(3), t, :], mv[:, j0, t, 0:1],
                                                       rstd[:, j0, t:t + 1], ALU.subtract, ALU.mult)
                    last.then_inc(s_xn, 1)
                if (s - 2).exists(GROUPS):
                    g = s - 2
                    need(dve, s_rms, g + 1)
                    need(dve, s_x1, g - 1)
                    for t in range(4):
                        last = nc.vector.scalar_tensor_tensor(out=Y[:, j0, t, :], in0=ps_h[:, j0, t * P:(t + 1) * P],
                                                              scalar=r_rms[:, t:t + 1], in1=scale_b[:, :],
                                                              op0=ALU.mult, op1=ALU.mult)
                    last.then_inc(s_y, 1)
                if (s - 0).exists(GROUPS):
                    g = s
                    need(dve, s_xhi, g + 1)
                    nc.vector.tensor_tensor(xt_lo[:, j0], ps_t[:, j0], xt_hi[:, j0].bitcast(fp32), ALU.subtract).then_inc(s_xlo, 1)
                if (s - 1).exists(GROUPS):
                    g = s - 1
                    need(dve, s_is, g + 1)
                    need(dve, s_zt, g + 1)
                    nc.vector.tensor_tensor(iz[:, :], i_s[:, :], z_tanh[:, j], ALU.mult).then_inc(s_iz, 1)
                    need(dve, s_fs, g + 1)
                    need(dve, s_nln, g)
                    for b in range(2):
                        q = slice(b * T, (b + 1) * T)
                        last = nc.vector.tensor_tensor_scan(N[:, q], f_s[:, q], i_s[:, q], 0.0, ALU.mult, ALU.add)
                    last.then_inc(s_cn, 1)
                    need(dve, s_iz, g + 1)
                    for b in range(2):
                        q = slice(b * T, (b + 1) * T)
                        last = nc.vector.tensor_tensor_scan(C[:, q], f_s[:, q], iz[:, q], 0.0, ALU.mult, ALU.add)
                    last.then_inc(s_cn, 1)
                    need(dve, s_cn, 2 * g + 2)
                    need(dve, s_ot, g + 1)
                    nc.vector.scalar_tensor_tensor(out=oc[:, :], in0=o_tanh[:, j], scalar=1.0, in1=C[:, :],
                                                   op0=ALU.add, op1=ALU.mult).then_inc(s_oc, 1)
                    need(dve, s_oc, g + 1)
                    need(dve, s_ninv, g + 1)
                    need(dve, s_ht, g - 1)
                    nc.vector.tensor_tensor(H2[:, j], oc[:, :], n_inv[:, :], ALU.mult).then_inc(s_h2, 1)

            steps(dve, GROUPS, 2, 6, step, 6)

        @block.tensor
        def _(pe):
            pe.wait_ge(s_prep, 6)

            def step(s):
                j, j0 = (s - 1).of(2), s.of(2)
                if (s - 0).exists(GROUPS):
                    g = s
                    need(pe, s_xn, g + 1)
                    need(pe, s_xlo, g - 1)
                    for t in range(4):
                        last = nc.tensor.transpose(ps_t[:, j0, t * P:(t + 1) * P], XN[:, j0, t, :], ident[:, :])
                    last.then_inc(s_xt, 1)
                if (s - 1).exists(GROUPS):
                    g = s - 1
                    need(pe, s_h2, g + 1)
                    need(pe, s_y, g - 1)
                    for t in range(4):
                        last = nc.tensor.transpose(ps_h[:, j, t * P:(t + 1) * P], H2[:, j, t * P:(t + 1) * P], ident[:, :])
                    last.then_inc(s_ht, 1)
                if (s - 0).exists(GROUPS):
                    g = s
                    need(pe, s_xlo, g + 1)
                    for c, freed in ((GI, s_it), (GF, s_sp), (GO, s_ot), (GZ, s_zt)):
                        need(pe, freed, g)
                        w = slice(c * D, (c + 1) * D)
                        nc.tensor.matmul(ps_g[:, c], w_lo[:, w], xt_hi[:, j0], start=True, stop=False)
                        nc.tensor.matmul(ps_g[:, c], w_hi[:, w], xt_lo[:, j0], start=False, stop=False)
                        nc.tensor.matmul(ps_g[:, c], w_hi[:, w], xt_hi[:, j0], start=False, stop=True).then_inc(s_g, 1)

            steps(pe, GROUPS, 2, 6, step, 6)

HEADS, HD = 16, 8
NG, NJ = 4, 4
PARTS = 3
ROWS = PARTS * HD
VW = 32
NEG = -1e30
NB = 4


def attention(nc, dram, const):
    x1_t = dram["x1"].rearrange("(b t p) d -> b p t d", p=P, t=2)
    h_t = dram["h"].rearrange("(b t p) d -> b p t d", p=P, t=2)
    q_scr, k_scr, m_scr = dram["q_scr"], dram["k_scr"], dram["m_scr"]
    ident, ident_b, mask_b = const["ident"], const["ident_b"], const["mask_b"]
    ctx = ExitStack()
    with ctx:
        def sb(name, shape, dt=fp32):
            return ctx.enter_context(nc.sbuf_tensor(name, shape, dt))

        def sem(name):
            return ctx.enter_context(nc.semaphore(name))

        w_f = sb("b_w_f", [P, 3 * D])
        w_hi = sb("b_w_hi", [P, 3 * D], f32r)
        w_lo = sb("b_w_lo", [P, 3 * D], f32r)
        wo = sb("b_wo", [P, D])
        g_b = sb("b_g", [P, 1, D])
        b_b = sb("b_b", [P, 1, D])
        eps_ln = sb("b_eps", [P, 1])
        zero_row = sb("b_zero", [16, T])
        X = sb("b_X", [P, NB, 2, D])
        stats = sb("b_stats", [P, 2, 6])
        mv = sb("b_mv", [P, 2, 2])
        lnv = sb("b_lnv", [P, 2])
        rstd = sb("b_rstd", [P, 2])
        XN = sb("b_XN", [P, NB, 2, D])
        xt_hi = sb("b_xt_hi", [P, T], f32r)
        xt_lo = sb("b_xt_lo", [P, T], f32r)
        qk_hi = sb("b_qk_hi", [P, 2, T], f32r)
        qk_lo = sb("b_qk_lo", [P, 2, T], f32r)
        V = sb("b_V", [P, NB, 2, HEADS, VW])
        Q = sb("b_Q", [P, NB, NJ, NG, T], f32r)
        K = sb("b_K", [P, NB, NG, T], f32r)
        m_neg = sb("b_m_neg", [P, 2, HEADS])
        mt = sb("b_mt", [HEADS, T], f32r)
        PT = sb("b_PT", [P, 2, 3, 512])
        OT = sb("b_OT", [P, 2, T])
        rec = sb("b_rec", [P, 2, NJ])
        attn = sb("b_attn", [P, 2, 2, NG, NJ, HD])
        at = sb("b_at", [P, T])
        R = sb("b_R", [P, 2, D])
        stats1 = sb("b_stats1", [P, 2, 6])
        mv1 = sb("b_mv1", [P, 2, 2])
        lnv1 = sb("b_lnv1", [P, 2])
        rstd1 = sb("b_rstd1", [P, 2])
        H0 = sb("b_H0", [P, 2, D])
        H1 = sb("b_H1", [P, 2, D])
        H = sb("b_H", [P, NB, 2, D])
        ps_s = ctx.enter_context(nc.psum_tensor("b_ps_s", [P, 3, 512], fp32))
        ps_m = ctx.enter_context(nc.psum_tensor("b_ps_m", [P, 2, 512], fp32))
        ps_o = ctx.enter_context(nc.psum_tensor("b_ps_o", [P, 2, T], fp32))
        ps_x = ctx.enter_context(nc.psum_tensor("b_ps_x", [P, 2, 512], fp32))

        s_load = sem("b_load")
        s_whi = sem("b_whi")
        s_prep = sem("b_prep")
        s_fill = sem("b_fill")
        s_x = [sem(f"b_x{k}") for k in range(NB)]
        s_st = sem("b_st")
        s_mv = sem("b_mvs")
        s_lnv = sem("b_lnvs")
        s_rstd = sem("b_rstds")
        s_xn = sem("b_xn")
        s_xt = sem("b_xt")
        s_xhi = sem("b_xhi")
        s_xlo = sem("b_xlo")
        s_qk = sem("b_qk")
        s_qkhi = sem("b_qkhi")
        s_qklo = sem("b_qklo")
        s_v = sem("b_v")
        s_vc = sem("b_vc")
        s_qkw = [sem(f"b_qkw{k}") for k in range(NB)]
        s_qkr = [sem(f"b_qkr{k}") for k in range(NB)]
        s_b = sem("b_b_s")
        s_red = sem("b_red")
        s_mt = sem("b_mts")
        s_mtc = sem("b_mtc")
        s_mw = [sem(f"b_mw{k}") for k in range(NB)]
        s_mr = [sem(f"b_mr{k}") for k in range(NB)]
        s_s = sem("b_s")
        s_e = sem("b_e")
        s_k = sem("b_k")
        s_pv = sem("b_pv")
        s_ot = sem("b_ot")
        s_ott = sem("b_ott")
        s_rec = sem("b_recs")
        s_att = sem("b_att")
        s_aT = sem("b_aT")
        s_at = sem("b_ats")
        s_wo = sem("b_wos")
        s_r = sem("b_r")
        s_st1 = sem("b_st1")
        s_mv1 = sem("b_mv1s")
        s_lnv1 = sem("b_lnv1s")
        s_rstd1 = sem("b_rstd1s")
        s_h0 = sem("b_h0")
        s_h1 = sem("b_h1")
        s_h = sem("b_h")
        s_out = [sem(f"b_out{k}") for k in range(NB)]
        block = ctx.enter_context(nc.Block())
        OB = [0, 0, 0, 1]
        WRITES, READS, MREADS = 6 * 16, 8 * 16, 4 * 16

        @block.sync
        def _(sync):
            sync.dma_start(w_f[:, :], dram["w_qkv"]).then_inc(s_load, 16)
            sync.dma_start(wo[:, :], dram["w_o"]).then_inc(s_load, 16)
            sync.dma_start(g_b[:, 0, :], dram["g1"].partition_broadcast(P)).then_inc(s_load, 16)
            sync.dma_start(b_b[:, 0, :], dram["b1"].partition_broadcast(P)).then_inc(s_load, 16)
            sync.wait_ge(s_fill, 1)
            for k in range(NB):
                sync.dma_start(q_scr[k, PARTS * P:, :], zero_row[:, :]).then_inc(s_load, 16)

            sync.wait_ge(s_fill, 4)

            def step(s):
                if s.exists(B):
                    b, n = s, s.of(NB)
                    need_apart(sync, (s_fill, 4), (s_xn, b - (NB - 1)))
                    sync.dma_start(X[:, n], x1_t[bass.ds(b.value(), 1)].rearrange("b p t d -> p (b t) d")).then_inc(s_x[n], 16)
                if (s - 1).exists(B):
                    b, n = s - 1, (s - 1).of(NB)
                    need(sync, s_qkr[n], b.turn(NB) * READS)
                    need(sync, s_qkhi, b + 1)
                    for part in (0, 1):
                        sync.dma_start(q_scr[n, part * P:(part + 1) * P, :], qk_hi[:, 0, :].bitcast(fp32)).then_inc(s_qkw[n], 16)
                    for part in (0, 2):
                        sync.dma_start(k_scr[n, part * P:(part + 1) * P, :], qk_hi[:, 1, :].bitcast(fp32)).then_inc(s_qkw[n], 16)
                    need(sync, s_qklo, b + 1)
                    sync.dma_start(q_scr[n, 2 * P:3 * P, :], qk_lo[:, 0, :].bitcast(fp32)).then_inc(s_qkw[n], 16)
                    sync.dma_start(k_scr[n, P:2 * P, :], qk_lo[:, 1, :].bitcast(fp32)).then_inc(s_qkw[n], 16)
                    need_apart(sync, (s_fill, 4), (s_qkw[n], b.turn(NB) * WRITES + WRITES), (s_s, (b - NB) * 12 + 12))
                    q_rows = q_scr[n].rearrange("(r g j) n -> j r g n", g=NG, j=NJ)
                    k_rows = k_scr[n].rearrange("(r g j) n -> j r g n", g=NG, j=NJ)
                    for j in range(NJ):
                        sync.dma_start(Q[32 * j:32 * j + ROWS + 1, n, j].bitcast(fp32), q_rows[j]).then_inc(s_qkr[n], 16)
                        sync.dma_start(K[32 * j:32 * j + ROWS, n].bitcast(fp32), k_rows[j]).then_inc(s_qkr[n], 16)
                if (s - 2).exists(B):
                    b, n = s - 2, (s - 2).of(NB)
                    need_apart(sync, (s_fill, 4), (s_mtc, b + 1), (s_mr[n], b.turn(NB) * MREADS))
                    sync.dma_start(m_scr[n], mt[:, :].bitcast(fp32)).then_inc(s_mw[n], 16)
                    need(sync, s_mw[n], b.turn(NB) * 16 + 16)
                    m_rows = m_scr[n].rearrange("(r g j) n -> j r g n", r=1, g=NG, j=NJ)
                    for j in range(NJ):
                        sync.dma_start(Q[32 * j + ROWS:32 * j + ROWS + 1, n, j].bitcast(fp32), m_rows[j]).then_inc(s_mr[n], 16)
                if (s - 4).exists(B):
                    b, n = s - 4, (s - 4).of(NB)
                    need_apart(sync, (s_fill, 4), (s_h, b + 1))
                    sync.dma_start(h_t[bass.ds(b.value(), 1)].rearrange("b p t d -> p (b t) d"), H[:, n]).then_inc(s_out[n], 16)

            sync.wait_ge(s_load, 16 * (4 + NB))
            steps(sync, B, 4, NB, step, 8)
            for k in range(NB):
                sync.wait_ge(s_out[k], 16 * len(range(k, B, NB)))

        @block.gpsimd
        def _(pool):
            nc.gpsimd.memset(zero_row[:, :], 0.0).then_inc(s_fill, 1)
            nc.gpsimd.memset(Q[:, :, :, :, :].bitcast(fp32), 0.0)
            nc.gpsimd.memset(V[:, :, :, :, :], 0.0).then_inc(s_fill, 1)
            pool.wait_ge(s_fill, 2)
            nc.gpsimd.memset(V[:, :, :, :, HD:HD + 1], 1.0).then_inc(s_fill, 1)
            nc.gpsimd.memset(K[:, :, :, :].bitcast(fp32), 1.0).then_inc(s_fill, 1)
            pool.wait_ge(s_fill, 4)

            def mask(b, g):
                for u in range(3):
                    need_apart(pool, (s_fill, 4), (s_e, 12 * b + (3 * g + u + 1)))
                    if u == 0:
                        tri = PT[:, g % 2, u].rearrange("p (j q) -> p j q", j=NJ)
                    else:
                        tri = PT[:, g % 2, u].rearrange("p (j q) -> p j q", j=2)[:, :, 0:P]
                    nc.gpsimd.affine_select(out=tri, in_=tri, compare_op=ALU.is_ge, fill=0.0, base=0,
                                            pattern=[[0, tri.shape[1]], [1, P]], channel_multiplier=-1).then_inc(s_k, 1)

            def step(s):
                c, d = s - 2, s - 3
                if c.exists(B):
                    for g in range(3):
                        mask(c, g)
                if d.exists(B):
                    n = d.of(NB)
                    need(pool, s_h0, d + 1)
                    nc.gpsimd.tensor_tensor(H1[:, :, :], H0[:, :, :], g_b[:, :, :].to_broadcast([P, 2, D]), ALU.mult).then_inc(s_h1, 1)
                    need(pool, s_h1, d + 1)
                    need(pool, s_out[n], d.turn(NB) * 16)
                    nc.gpsimd.tensor_tensor(H[:, n], H1[:, :, :], b_b[:, :, :].to_broadcast([P, 2, D]), ALU.add).then_inc(s_h, 1)
                if c.exists(B):
                    mask(c, 3)

            steps(pool, B, 3, NB, step, 8)

        @block.scalar
        def _(act):
            act.wait_ge(s_load, 16 * (4 + NB))
            for c in range(2):
                w = slice(c * D, (c + 1) * D)
                nc.scalar.copy(w_hi[:, w].rearrange("p (r h) -> p r h", h=HEADS), w_f[:, w].rearrange("p (h r) -> p r h", h=HEADS))
            nc.scalar.copy(w_hi[:, 2 * D:], w_f[:, 2 * D:]).then_inc(s_whi, 1)
            act.wait_ge(s_fill, 4)
            act.wait_ge(s_prep, 1)

            def exps(b, g):
                for u in range(3):
                    need(act, s_s, 12 * b + (3 * g + u + 1))
                    need(act, s_pv, 4 * b + (g - 1))
                    nc.scalar.activation(PT[:, g % 2, u], ps_s[:, u], ACT.Exp, scale=HD ** -0.5).then_inc(s_e, 1)

            def evac_o(b, g):
                need(act, s_pv, 4 * b + (g + 1))
                need(act, s_ott, 4 * b + (g - 1))
                nc.scalar.copy(OT[:, g % 2], ps_o[:, g % 2]).then_inc(s_ot, 1)

            def step(s):
                a, b2, c, d = s, s - 1, s - 2, s - 3
                A, BB, C, DD = a.exists(B), b2.exists(B), c.exists(B), d.exists(B)
                if A:
                    need(act, s_mv, a + 1)
                    need(act, s_rstd, a)
                    nc.scalar.activation(lnv[:, :], mv[:, :, 1], ACT.Ln, bias=eps_ln[:, :]).then_inc(s_lnv, 1)
                    need(act, s_lnv, a + 1)
                    need(act, s_xn, a)
                    nc.scalar.activation(rstd[:, :], lnv[:, :], ACT.Exp, scale=-0.5).then_inc(s_rstd, 1)
                if C:
                    exps(c, 0)
                if DD:
                    need(act, s_aT, d + 1)
                    need(act, s_wo, d)
                    nc.scalar.copy(at[:, :], ps_x[:, 0, 0:T]).then_inc(s_at, 1)
                if A:
                    need(act, s_xt, a + 1)
                    need(act, s_v, a)
                    nc.scalar.copy(xt_hi[:, :], ps_x[:, 1, 0:T]).then_inc(s_xhi, 1)
                if C:
                    exps(c, 1)
                if DD:
                    need(act, s_mv1, d + 1)
                    need(act, s_rstd1, d)
                    nc.scalar.activation(lnv1[:, :], mv1[:, :, 1], ACT.Ln, bias=eps_ln[:, :]).then_inc(s_lnv1, 1)
                    need(act, s_lnv1, d + 1)
                    need(act, s_h0, d)
                    nc.scalar.activation(rstd1[:, :], lnv1[:, :], ACT.Exp, scale=-0.5).then_inc(s_rstd1, 1)
                if A:
                    need(act, s_qk, a + 1)
                    need(act, s_qkw[(a - 1).of(NB)], (a - 1).turn(NB) * WRITES + WRITES)
                    need(act, s_qklo, a)
                    nc.scalar.copy(qk_hi[:, :, :].rearrange("p a n -> p (a n)"), ps_x[:, 1]).then_inc(s_qkhi, 1)
                if C:
                    evac_o(c, 0)
                    exps(c, 2)
                if A:
                    need(act, s_v, a + 1)
                    need(act, s_pv, 4 * (a - NB) + 4)
                    nc.scalar.copy(V[:, a.of(NB), :, :, 0:HD], ps_x[:, 1, 0:T].rearrange("p (t h r) -> p t h r", t=2, h=HEADS)).then_inc(s_vc, 1)
                if C:
                    evac_o(c, 1)
                    exps(c, 3)
                    evac_o(c, 2)
                if BB:
                    need(act, s_mt, b2 + 1)
                    need(act, s_mw[(b2 - 1).of(NB)], (b2 - 1).turn(NB) * 16 + 16)
                    nc.scalar.copy(mt[:, :], ps_x[0:HEADS, 0, 0:T]).then_inc(s_mtc, 1)
                if C:
                    evac_o(c, 3)

            steps(act, B, 3, NB, step, 8)

        @block.vector
        def _(dve):
            nc.vector.memset(eps_ln[:, :], LN_EPS).then_inc(s_prep, 1)
            dve.wait_ge(s_whi, 1)
            for c in range(2):
                w = slice(c * D, (c + 1) * D)
                nc.vector.tensor_tensor(w_lo[:, w].rearrange("p (r h) -> p r h", h=HEADS), w_f[:, w].rearrange("p (h r) -> p r h", h=HEADS),
                                        w_hi[:, w].bitcast(fp32).rearrange("p (r h) -> p r h", h=HEADS), ALU.subtract)
            nc.vector.tensor_tensor(w_lo[:, 2 * D:], w_f[:, 2 * D:], w_hi[:, 2 * D:].bitcast(fp32), ALU.subtract).then_inc(s_prep, 1)

            def reduces(b, n):
                for u in range(3 * n, 3 * n + 3):
                    need(dve, s_b, 12 * b + (u + 1))
                    need(dve, s_mt, b)
                    if u < 4:
                        scores, out = ps_m[:, u % 2].rearrange("p (j k) -> p j k", j=4), m_neg[:, 0, 4 * u:4 * u + 4]
                    else:
                        scores, out = ps_m[:, u % 2].rearrange("p (j k) -> p j k", j=2), m_neg[:, 1, 2 * u - 8:2 * u - 6]
                    nc.vector.tensor_reduce(out, scores, AX.X, ALU.max, negate=True).then_inc(s_red, 1)

            def norm_o(b, g):
                need(dve, s_ott, 4 * b + (g + 1))
                need(dve, s_att, 4 * b + g)
                o = ps_x[:, OB[g], 0:T].rearrange("p (t j r) -> p t j r", t=2, j=NJ)
                nc.vector.reciprocal(rec[:, :, :], o[:, :, :, HD]).then_inc(s_rec, 1)
                need(dve, s_rec, 4 * b + (g + 1))
                need(dve, s_aT, b - 1)
                nc.vector.tensor_tensor(attn[:, b.of(2), :, g], o[:, :, :, 0:HD],
                                        rec[:, :, :].unsqueeze(3).to_broadcast([P, 2, NJ, HD]), ALU.mult).then_inc(s_att, 1)

            def step(s):
                a, b2, c, d = s, s - 1, s - 2, s - 3
                A, BB, C, DD = a.exists(B), b2.exists(B), c.exists(B), d.exists(B)
                if A:
                    n = a.of(NB)
                    need(dve, s_x[n], a.turn(NB) * 16 + 16)
                    need(dve, s_mv, a)
                    for t in range(2):
                        last = nc.vector.bn_stats(stats[:, t, :], X[:, n, t, :])
                    last.then_inc(s_st, 1)
                    need_apart(dve, (s_prep, 1), (s_st, a + 1), (s_xn, a))
                    for t in range(2):
                        last = nc.vector.bn_aggr(mv[:, t, :], stats[:, t, :])
                    last.then_inc(s_mv, 1)
                if BB:
                    reduces(b2, 0)
                if A:
                    need(dve, s_rstd, a + 1)
                    need(dve, s_r, a - 3)
                    for t in range(2):
                        last = nc.vector.tensor_scalar(XN[:, a.of(NB), t, :], X[:, n, t, :], mv[:, t, 0:1],
                                                       rstd[:, t:t + 1], ALU.subtract, ALU.mult)
                    last.then_inc(s_xn, 1)
                    need(dve, s_xhi, a + 1)
                    nc.vector.tensor_tensor(xt_lo[:, :], ps_x[:, 1, 0:T], xt_hi[:, :].bitcast(fp32), ALU.subtract).then_inc(s_xlo, 1)
                if BB:
                    reduces(b2, 1)
                if DD:
                    need(dve, s_wo, d + 1)
                    need(dve, s_h0, d)
                    nc.vector.tensor_tensor(R[:, :, :], ps_x[:, 0, 0:T].rearrange("p (t d) -> p t d", t=2), XN[:, d.of(NB)], ALU.add).then_inc(s_r, 1)
                    need(dve, s_r, d + 1)
                    for t in range(2):
                        last = nc.vector.bn_stats(stats1[:, t, :], R[:, t, :])
                    last.then_inc(s_st1, 1)
                    need_apart(dve, (s_prep, 1), (s_st1, d + 1), (s_lnv1, d))
                    for t in range(2):
                        last = nc.vector.bn_aggr(mv1[:, t, :], stats1[:, t, :])
                    last.then_inc(s_mv1, 1)
                if A:
                    need(dve, s_qkhi, a + 1)
                    need(dve, s_qkw[(a - 1).of(NB)], (a - 1).turn(NB) * WRITES + WRITES)
                    nc.vector.tensor_tensor(qk_lo[:, :, :].rearrange("p a n -> p (a n)"), ps_x[:, 1],
                                            qk_hi[:, :, :].bitcast(fp32).rearrange("p a n -> p (a n)"), ALU.subtract).then_inc(s_qklo, 1)
                if C:
                    norm_o(c, 0)
                if BB:
                    reduces(b2, 2)
                if DD:
                    need(dve, s_rstd1, d + 1)
                    need(dve, s_h1, d)
                    for t in range(2):
                        last = nc.vector.tensor_scalar(H0[:, t, :], R[:, t, :], mv1[:, t, 0:1],
                                                       rstd1[:, t:t + 1], ALU.subtract, ALU.mult)
                    last.then_inc(s_h0, 1)
                if C:
                    norm_o(c, 1)
                if BB:
                    reduces(b2, 3)
                if C:
                    norm_o(c, 2)
                    norm_o(c, 3)

            steps(dve, B, 3, NB, step, 8)

        @block.tensor
        def _(pe):
            pe.wait_ge(s_prep, 2)

            def scores(c, g):
                n = c.of(NB)
                if g == 0:
                    need(pe, s_mr[n], c.turn(NB) * MREADS + MREADS)
                need(pe, s_e, 12 * c + (3 * g - 2))
                nc.tensor.matmul(ps_s[:, 0].rearrange("p (j q) -> p j q", j=NJ), K[:, n, g, P:T], Q[:, n, :, g, P:T],
                                 start=True, stop=True).then_inc(s_s, 1)
                for u in (1, 2):
                    need(pe, s_e, 12 * c + (3 * g - 2 + u))
                    nc.tensor.matmul(ps_s[:, u].rearrange("p (j q) -> p j q", j=2), K[:, n, g, 0:P], Q[:, n, 2 * u - 2:2 * u, g, :],
                                     start=True, stop=True).then_inc(s_s, 1)

            def maxima(b, m):
                n = b.of(NB)
                if m == 0:
                    need(pe, s_qkr[n], b.turn(NB) * READS + READS)
                for u in range(3 * m, 3 * m + 3):
                    need(pe, s_red, 12 * b + (u - 1))
                    if u < 4:
                        nc.tensor.matmul(ps_m[:, u % 2].rearrange("p (j k) -> p j k", j=4), ident_b[:, :], mask_b[:, :, :],
                                         start=True, stop=False, skip_group_check=True)
                        for j in range(4):
                            last = nc.tensor.matmul(ps_m[:, u % 2, j * P:(j + 1) * P], Q[:, n, j, u, 0:P], K[:, n, u, 0:P],
                                                    start=False, stop=(j == 3), skip_group_check=True)
                    else:
                        g, jp = divmod(u - 4, 2)
                        nc.tensor.matmul(ps_m[:, u % 2].rearrange("p (j k) -> p j k", j=2)[:, :, P:T], ident_b[:, :], mask_b[:, 0:2, :],
                                         start=True, stop=False, skip_group_check=True)
                        for j in range(2):
                            last = nc.tensor.matmul(ps_m[:, u % 2, j * T:(j + 1) * T], Q[:, n, 2 * jp + j, g, P:T], K[:, n, g, :],
                                                    start=False, stop=(j == 1), skip_group_check=True)
                    last.then_inc(s_b, 1)

            def values(c, g):
                n = c.of(NB)
                need(pe, s_k, 12 * c + (3 * g + 3))
                need(pe, s_ot, 4 * c + (g - 1))
                for j in range(NJ):
                    h = 4 * g + j
                    nc.tensor.matmul(ps_o[32 * j:32 * j + VW, g % 2, :], V[:, n, 0, h, :],
                                     PT[:, g % 2, 1 + j // 2, (j % 2) * T:(j % 2 + 1) * T], start=True, stop=False, skip_group_check=True)
                for j in range(NJ):
                    h = 4 * g + j
                    last = nc.tensor.matmul(ps_o[32 * j:32 * j + VW, g % 2, P:T], V[:, n, 1, h, :],
                                            PT[:, g % 2, 0, j * P:(j + 1) * P], start=False, stop=True, skip_group_check=True)
                last.then_inc(s_pv, 1)

            def o_rows(c, g):
                need(pe, s_ot, 4 * c + (g + 1))
                for t in range(2):
                    last = nc.tensor.transpose(ps_x[:, OB[g], t * P:(t + 1) * P], OT[:, g % 2, t * P:(t + 1) * P], ident[:, :])
                last.then_inc(s_ott, 1)

            def step(s):
                a, b2, c, d = s, s - 1, s - 2, s - 3
                A, BB, C, DD = a.exists(B), b2.exists(B), c.exists(B), d.exists(B)
                if C:
                    scores(c, 0)
                if BB:
                    maxima(b2, 0)
                if DD:
                    need(pe, s_att, 4 * d + 4)
                    need(pe, s_mtc, b2.most(B))
                    for t in range(2):
                        last = nc.tensor.transpose(ps_x[:, 0, t * P:(t + 1) * P],
                                                   attn[:, d.of(2), t].rearrange("p g j r -> p (g j r)"), ident[:, :])
                    last.then_inc(s_aT, 1)
                if A:
                    need(pe, s_xn, a + 1)
                    need(pe, s_vc, a)
                    need(pe, s_att, 4 * c)
                    for t in range(2):
                        last = nc.tensor.transpose(ps_x[:, 1, t * P:(t + 1) * P], XN[:, a.of(NB), t, :], ident[:, :])
                    last.then_inc(s_xt, 1)
                if C:
                    scores(c, 1)
                    values(c, 0)
                if BB:
                    maxima(b2, 1)
                if DD:
                    need(pe, s_at, d + 1)
                    for t in range(2):
                        last = nc.tensor.matmul(ps_x[:, 0, t * P:(t + 1) * P], at[:, t * P:(t + 1) * P], wo[:, :], start=True, stop=True)
                    last.then_inc(s_wo, 1)
                if A:
                    need(pe, s_xlo, a + 1)
                    for i in range(2):
                        w, out = slice(i * D, (i + 1) * D), ps_x[:, 1, i * T:(i + 1) * T]
                        nc.tensor.matmul(out, w_lo[:, w], xt_hi[:, :], start=True, stop=False)
                        nc.tensor.matmul(out, w_hi[:, w], xt_lo[:, :], start=False, stop=False)
                        last = nc.tensor.matmul(out, w_hi[:, w], xt_hi[:, :], start=False, stop=True)
                    last.then_inc(s_qk, 1)
                if C:
                    need(pe, s_r, d + 1)
                    need(pe, s_mtc, c + 1)
                    o_rows(c, 0)
                    scores(c, 2)
                    values(c, 1)
                if BB:
                    maxima(b2, 2)
                if A:
                    need(pe, s_qklo, a + 1)
                    for t in range(2):
                        x, out = slice(t * P, (t + 1) * P), ps_x[:, 1, t * P:(t + 1) * P]
                        nc.tensor.matmul(out, xt_hi[:, x], w_lo[:, 2 * D:], start=True, stop=False)
                        nc.tensor.matmul(out, xt_lo[:, x], w_hi[:, 2 * D:], start=False, stop=False)
                        last = nc.tensor.matmul(out, xt_hi[:, x], w_hi[:, 2 * D:], start=False, stop=True)
                    last.then_inc(s_v, 1)
                if C:
                    need(pe, s_att, 4 * c + 1)
                    o_rows(c, 1)
                    scores(c, 3)
                    values(c, 2)
                if BB:
                    maxima(b2, 3)
                if C:
                    need(pe, s_att, 4 * c + 2)
                    o_rows(c, 2)
                    need(pe, s_vc, c + 1)
                    values(c, 3)
                if BB:
                    need(pe, s_att, 4 * c + 3)
                    need(pe, s_red, 12 * b2 + 12)
                    for t in range(2):
                        last = nc.tensor.transpose(ps_x[0:HEADS, 0, t * P:(t + 1) * P], m_neg[:, t, :], ident[:, :])
                    last.then_inc(s_mt, 1)
                if C:
                    need(pe, s_vc, (a + 1).most(B))
                    need(pe, s_att, 4 * c)
                    o_rows(c, 3)

            steps(pe, B, 3, NB, step, 8)


E, F = 8, 512
NF = F // P


def experts(nc, dram, const):
    GROUPS = NTILE // 4
    x1_t = dram["x1"].rearrange("(t p) d -> p t d", p=P)
    h_t = dram["h"].rearrange("(t p) d -> p t d", p=P)
    out_t = dram["out"].rearrange("b (h p) d -> p (b h) d", p=P)
    ident = const["ident"]
    ctx = ExitStack()
    with ctx:
        def sb(name, shape, dt=fp32):
            return ctx.enter_context(nc.sbuf_tensor(name, shape, dt))

        def sem(name):
            return ctx.enter_context(nc.semaphore(name))

        w1_f = sb("c_w1_f", [P, F])
        w1_hi = sb("c_w1_hi", [P, E, F], f32r)
        w1_lo = sb("c_w1_lo", [P, E, F], f32r)
        w2 = sb("c_w2", [P, E, NF, D])
        wg_f = sb("c_wg_f", [P, E])
        bb1 = sb("c_bb1", [P, E, NF])
        bb2 = sb("c_bb2", [E, D])
        g_b = sb("c_g", [P, 1, D])
        b_b = sb("c_b", [P, 1, D])
        eps_ln = sb("c_eps", [P, 1])
        iota = sb("c_iota", [P, E])
        X = sb("c_X", [P, 2, 4, D])
        H = sb("c_H", [P, 2, 4, D])
        ht = sb("c_ht", [P, 2, 512])
        ht_hi = sb("c_ht_hi", [P, 2, 512], f32r)
        ht_lo = sb("c_ht_lo", [P, 2, 512], f32r)
        logits = sb("c_logits", [P, 4, E])
        top = sb("c_top", [P, 4, E])
        idx = sb("c_idx", [P, 4, E], u32)
        idx_f = sb("c_idx_f", [P, 4, 2])
        gap = sb("c_gap", [P, 4])
        e1 = sb("c_e1", [P, 4])
        den = sb("c_den", [P, 4])
        wt = sb("c_wt", [P, 4, 2])
        wa = sb("c_wa", [P, 4, E])
        w = sb("c_w", [P, 2, 4, E])
        wT = sb("c_wT", [E, 512])
        h1 = sb("c_h1", [P, 4, 512])
        acc = sb("c_acc", [P, 2, 4, D])
        stats = sb("c_stats", [P, 4, 6])
        mv = sb("c_mv", [P, 4, 2])
        lnv = sb("c_lnv", [P, 4])
        rstd = sb("c_rstd", [P, 4])
        Y0 = sb("c_Y0", [P, 4, D])
        Y1 = sb("c_Y1", [P, 4, D])
        Y2 = sb("c_Y2", [P, 4, D])
        Y3 = sb("c_Y3", [P, 2, 4, D])
        ps_t = ctx.enter_context(nc.psum_tensor("c_ps_t", [P, 512], fp32))
        ps_l = ctx.enter_context(nc.psum_tensor("c_ps_l", [P, 512], fp32))
        ps_1 = ctx.enter_context(nc.psum_tensor("c_ps_1", [P, 4, 512], fp32))
        ps_2 = ctx.enter_context(nc.psum_tensor("c_ps_2", [P, 2, 512], fp32))

        names = ("load w1f w1hi w1lo eps iota t ht hthi htlo l lg top idx idxf gap e1 den w0 w1 wa w wT wTc a h1 y acc b2 accb st mv "
                 "lnv rstd y0 y1 y2 y3").split()
        S = {n: sem("c_" + n) for n in names}
        s_in = [sem(f"c_in{k}") for k in range(2)]
        s_out = [sem(f"c_out{k}") for k in range(2)]
        block = ctx.enter_context(nc.Block())

        @block.sync
        def _(sync):
            sync.dma_start(wg_f[:, :], dram["wg"]).then_inc(S["load"], 16)
            sync.dma_start(w2[:, :, :, :], dram["w2"].rearrange("e (c p) d -> p e c d", p=P)).then_inc(S["load"], 16)
            sync.dma_start(bb1[:, :, :], dram["bb1"].rearrange("e (c p) -> p e c", p=P), allow_slow_non_contiguous=True).then_inc(S["load"], 16)
            sync.dma_start(bb2[:, :], dram["bb2"]).then_inc(S["load"], 16)
            sync.dma_start(g_b[:, 0, :], dram["g2"].partition_broadcast(P)).then_inc(S["load"], 16)
            sync.dma_start(b_b[:, 0, :], dram["b2"].partition_broadcast(P)).then_inc(S["load"], 16)
            for e in range(E):
                if e:
                    sync.wait_ge(S["w1lo"], e)
                sync.dma_start(w1_f[:, :], dram["w1"][e]).then_inc(S["w1f"], 16)

            sync.wait_ge(S["load"], 96)

            def step(s):
                if s.exists(GROUPS):
                    n = s.of(2)
                    need_apart(sync, (S["load"], 96), (S["y3"], s - 1))
                    sync.dma_start(H[:, n], h_t[:, bass.ds((s * 4).value(), 4), :]).then_inc(s_in[n], 16)
                    sync.dma_start(X[:, n], x1_t[:, bass.ds((s * 4).value(), 4), :]).then_inc(s_in[n], 16)
                if (s - 1).exists(GROUPS):
                    g = s - 1
                    need_apart(sync, (S["load"], 96), (S["y3"], g + 1))
                    sync.dma_start(out_t[:, bass.ds((g * 4).value(), 4), :], Y3[:, g.of(2)]).then_inc(s_out[g.of(2)], 16)

            steps(sync, GROUPS, 1, 2, step, 4)
            for k in range(2):
                sync.wait_ge(s_out[k], 16 * GROUPS // 2)

        @block.gpsimd
        def _(pool):
            nc.gpsimd.iota(iota[:, :], pattern=[[1, E]], base=0, channel_multiplier=0, allow_small_or_imprecise_dtypes=True).then_inc(S["iota"], 1)
            pool.wait_ge(S["load"], 96)

            def step(s):
                g, n = s, s.of(2)
                need(pool, S["y0"], g + 1)
                need(pool, S["y2"], g)
                nc.gpsimd.tensor_tensor(Y1[:, :, :], Y0[:, :, :], g_b[:, :, :].to_broadcast([P, 4, D]), ALU.mult).then_inc(S["y1"], 1)
                need(pool, S["y1"], g + 1)
                nc.gpsimd.tensor_tensor(Y2[:, :, :], Y1[:, :, :], b_b[:, :, :].to_broadcast([P, 4, D]), ALU.add).then_inc(S["y2"], 1)
                need(pool, S["y2"], g + 1)
                need(pool, s_out[n], g.turn(2) * 16)
                nc.gpsimd.tensor_tensor(Y3[:, n], Y2[:, :, :], X[:, n], ALU.add).then_inc(S["y3"], 1)

            steps(pool, GROUPS, 0, 2, step, 2)

        @block.scalar
        def _(act):
            for e in range(E):
                act.wait_ge(S["w1f"], 16 * e + 16)
                nc.scalar.copy(w1_hi[:, e, :], w1_f[:, :]).then_inc(S["w1hi"], 1)
            act.wait_ge(S["load"], 96)
            act.wait_ge(S["eps"], 1)

            def step(s):
                g, n = s, s.of(2)
                need(act, S["t"], g + 1)
                nc.scalar.copy(ht_hi[:, n], ps_t[:, :]).then_inc(S["hthi"], 1)
                nc.scalar.copy(ht[:, n], ps_t[:, :]).then_inc(S["ht"], 1)
                need(act, S["gap"], g + 1)
                nc.scalar.activation(e1[:, :], gap[:, :], ACT.Exp).then_inc(S["e1"], 1)
                need(act, S["wT"], g + 1)
                nc.scalar.copy(wT[:, :], ps_l[0:E, :]).then_inc(S["wTc"], 1)
                for e in range(E):
                    for c in range(NF):
                        q = 4 * e + c
                        need(act, S["a"], 32 * g + (q + 1))
                        need(act, S["y"], 32 * g + (q - 3))
                        nc.scalar.activation(h1[:, c], ps_1[:, c], ACT.Gelu_apprx_tanh, bias=bb1[:, e, c:c + 1]).then_inc(S["h1"], 1)
                need(act, S["mv"], g + 1)
                nc.scalar.activation(lnv[:, :], mv[:, :, 1], ACT.Ln, bias=eps_ln[:, :]).then_inc(S["lnv"], 1)
                need(act, S["lnv"], g + 1)
                nc.scalar.activation(rstd[:, :], lnv[:, :], ACT.Exp, scale=-0.5).then_inc(S["rstd"], 1)

            steps(act, GROUPS, 0, 2, step, 2)

        @block.vector
        def _(dve):
            nc.vector.memset(eps_ln[:, :], LN_EPS).then_inc(S["eps"], 1)
            for e in range(E):
                dve.wait_ge(S["w1hi"], e + 1)
                nc.vector.tensor_tensor(w1_lo[:, e, :], w1_f[:, :], w1_hi[:, e, :].bitcast(fp32), ALU.subtract).then_inc(S["w1lo"], 1)
            dve.wait_ge(S["iota"], 1)

            def step(s):
                g, n = s, s.of(2)
                need(dve, S["hthi"], g + 1)
                need(dve, S["ht"], g + 1)
                nc.vector.tensor_tensor(ht_lo[:, n], ps_t[:, :], ht_hi[:, n].bitcast(fp32), ALU.subtract).then_inc(S["htlo"], 1)
                need(dve, S["l"], g + 1)
                nc.vector.tensor_copy(logits[:, :, :], ps_l[:, 0:4 * E].rearrange("p (t e) -> p t e", e=E)).then_inc(S["lg"], 1)
                need_apart(dve, (S["iota"], 1), (S["lg"], g + 1))
                for t in range(4):
                    last = nc.vector.max(top[:, t, :], logits[:, t, :])
                last.then_inc(S["top"], 1)
                need_apart(dve, (S["iota"], 1), (S["top"], g + 1))
                for t in range(4):
                    last = nc.vector.max_index(idx[:, t, :], top[:, t, :], logits[:, t, :])
                last.then_inc(S["idx"], 1)
                nc.vector.tensor_tensor(gap[:, :], top[:, :, 1], top[:, :, 0], ALU.subtract).then_inc(S["gap"], 1)
                need(dve, S["idx"], g + 1)
                nc.vector.tensor_copy(idx_f[:, :, :], idx[:, :, 0:2]).then_inc(S["idxf"], 1)
                need(dve, S["e1"], g + 1)
                nc.vector.tensor_scalar(den[:, :], e1[:, :], 1.0, None, ALU.add).then_inc(S["den"], 1)
                need(dve, S["den"], g + 1)
                nc.vector.reciprocal(wt[:, :, 0], den[:, :]).then_inc(S["w0"], 1)
                need(dve, S["w0"], g + 1)
                nc.vector.tensor_tensor(wt[:, :, 1], wt[:, :, 0], e1[:, :], ALU.mult).then_inc(S["w1"], 1)
                need(dve, S["w1"], g + 1)
                need(dve, S["idxf"], g + 1)
                for t in range(4):
                    last = nc.vector.tensor_scalar(wa[:, t, :], iota[:, :], idx_f[:, t, 0:1], wt[:, t, 0:1], ALU.is_equal, ALU.mult)
                last.then_inc(S["wa"], 1)
                for t in range(4):
                    last = nc.vector.tensor_scalar(logits[:, t, :], iota[:, :], idx_f[:, t, 1:2], wt[:, t, 1:2], ALU.is_equal, ALU.mult)
                last.then_inc(S["wa"], 1)
                need(dve, S["wa"], 2 * g + 2)
                nc.vector.tensor_tensor(w[:, n], wa[:, :, :], logits[:, :, :], ALU.add).then_inc(S["w"], 1)
                need(dve, S["b2"], g + 1)
                nc.vector.tensor_tensor(acc[:, 1], ps_l[:, :].rearrange("p (t d) -> p t d", t=4), H[:, n], ALU.add).then_inc(S["accb"], 1)
                need(dve, S["w"], g + 1)
                need(dve, S["accb"], g + 1)
                for e in range(E):
                    need(dve, S["y"], 32 * g + (4 * e + 4))
                    need(dve, S["acc"], 8 * g + e)
                    for t in range(4):
                        last = nc.vector.scalar_tensor_tensor(out=acc[:, e % 2, t, :], in0=ps_2[:, e % 2, t * P:(t + 1) * P],
                                                              scalar=w[:, n, t, e:e + 1], in1=acc[:, (e + 1) % 2, t, :],
                                                              op0=ALU.mult, op1=ALU.add)
                    last.then_inc(S["acc"], 1)
                need(dve, S["acc"], 8 * g + 8)
                for t in range(4):
                    last = nc.vector.bn_stats(stats[:, t, :], acc[:, 1, t, :])
                last.then_inc(S["st"], 1)
                need_apart(dve, (S["iota"], 1), (S["st"], g + 1))
                for t in range(4):
                    last = nc.vector.bn_aggr(mv[:, t, :], stats[:, t, :])
                last.then_inc(S["mv"], 1)
                need(dve, S["rstd"], g + 1)
                need(dve, S["y1"], g)
                for t in range(4):
                    last = nc.vector.tensor_scalar(Y0[:, t, :], acc[:, 1, t, :], mv[:, t, 0:1], rstd[:, t:t + 1], ALU.subtract, ALU.mult)
                last.then_inc(S["y0"], 1)

            steps(dve, GROUPS, 0, 2, step, 2)

        @block.tensor
        def _(pe):
            pe.wait_ge(S["w1lo"], E)
            pe.wait_ge(S["load"], 96)

            def step(s):
                g, n = s, s.of(2)
                need(pe, s_in[n], g.turn(2) * 32 + 32)
                need(pe, S["htlo"], g)
                need(pe, S["ht"], g)
                for t in range(4):
                    last = nc.tensor.transpose(ps_t[:, t * P:(t + 1) * P], H[:, n, t, :], ident[:, :])
                last.then_inc(S["t"], 1)
                need(pe, S["ht"], g + 1)
                need(pe, S["accb"], g)
                for t in range(4):
                    last = nc.tensor.matmul(ps_l[:, t * E:(t + 1) * E], ht[:, n, t * P:(t + 1) * P], wg_f[:, :], start=True, stop=True)
                last.then_inc(S["l"], 1)
                need(pe, S["w"], g + 1)
                for t in range(4):
                    last = nc.tensor.transpose(ps_l[0:E, t * P:(t + 1) * P], w[:, n, t, :], ident[:, :])
                last.then_inc(S["wT"], 1)
                need(pe, S["wTc"], g + 1)
                for t in range(4):
                    last = nc.tensor.matmul(ps_l[:, t * P:(t + 1) * P], wT[:, t * P:(t + 1) * P], bb2[:, :], start=True, stop=True)
                last.then_inc(S["b2"], 1)
                need(pe, S["htlo"], g + 1)

                def down(e):
                    need(pe, S["acc"], 8 * g + (e - 1))
                    for c in range(NF):
                        need(pe, S["h1"], 32 * g + (4 * e + c + 1))
                        for t in range(4):
                            last = nc.tensor.matmul(ps_2[:, e % 2, t * P:(t + 1) * P], h1[:, c, t * P:(t + 1) * P], w2[:, e, c, :],
                                                    start=(c == 0 and t == 0), stop=(c == NF - 1), skip_group_check=True)
                        last.then_inc(S["y"], 1)

                for e in range(E):
                    for c in range(NF):
                        q = 4 * e + c
                        need(pe, S["h1"], 32 * g + (q - 3))
                        wc = slice(c * P, (c + 1) * P)
                        nc.tensor.matmul(ps_1[:, c], w1_lo[:, e, wc], ht_hi[:, n], start=True, stop=False)
                        nc.tensor.matmul(ps_1[:, c], w1_hi[:, e, wc], ht_lo[:, n], start=False, stop=False)
                        nc.tensor.matmul(ps_1[:, c], w1_hi[:, e, wc], ht_hi[:, n], start=False, stop=True).then_inc(S["a"], 1)
                    if e:
                        down(e - 1)
                down(E - 1)

            steps(pe, GROUPS, 0, 2, step, 2)


def constants(nc, ctx):
    ident = ctx.enter_context(nc.sbuf_tensor("ident", [P, P], fp32))
    ident_b = ctx.enter_context(nc.sbuf_tensor("ident_b", [P, P], bf16))
    mask_b = ctx.enter_context(nc.sbuf_tensor("mask_b", [P, 4, P], bf16))
    s_zero = ctx.enter_context(nc.semaphore("s_zero"))
    with nc.Block() as block:

        @block.gpsimd
        def _(pool):
            nc.gpsimd.memset(ident[:, :], 0.0)
            nc.gpsimd.memset(ident_b[:, :], 0.0)
            nc.gpsimd.memset(mask_b[:, :, :], 0.0).then_inc(s_zero, 1)
            pool.wait_ge(s_zero, 1)
            for m in (ident, ident_b):
                nc.gpsimd.affine_select(out=m[:, :], in_=m[:, :], compare_op=ALU.not_equal, fill=1.0, base=0,
                                        pattern=[[-1, P]], channel_multiplier=1)
            nc.gpsimd.affine_select(out=mask_b[:, :, :], in_=mask_b[:, :, :], compare_op=ALU.is_ge, fill=NEG, base=0,
                                    pattern=[[0, 4], [-1, P]], channel_multiplier=1).then_inc(s_zero, 1)
            pool.wait_ge(s_zero, 2)

    return dict(ident=ident, ident_b=ident_b, mask_b=mask_b)


def build(nc, dram):
    dram["x1"] = nc.dram_tensor("x1", (B * T, D), fp32).ap()
    dram["h"] = nc.dram_tensor("h", (B * T, D), fp32).ap()
    dram["q_scr"] = nc.dram_tensor("q_scr", (NB, PARTS * P + HEADS, T), fp32).ap()
    dram["k_scr"] = nc.dram_tensor("k_scr", (NB, PARTS * P, T), fp32).ap()
    dram["m_scr"] = nc.dram_tensor("m_scr", (NB, HEADS, T), fp32).ap()
    with ExitStack() as ctx:
        const = constants(nc, ctx)
        recurrent_layer(nc, dram, const)
        attention(nc, dram, const)
        experts(nc, dram, const)


_INS = {
    "L0_attn_x": "x", "L0_attn_W": "W", "L0_attn_b": "b", "L0_attn_input_bias": "input_bias", "L0_attn_scale": "scale",
    "L0_ffn_w_qkv": "w_qkv", "L0_ffn_w_o": "w_o", "L0_ffn_g1": "g1", "L0_ffn_b1": "b1", "L0_ffn_wg": "wg",
    "L0_ffn_w1": "w1", "L0_ffn_bb1": "bb1", "L0_ffn_w2": "w2", "L0_ffn_bb2": "bb2", "L0_ffn_g2": "g2", "L0_ffn_b2": "b2",
}


def kernel(**inputs):
    import numpy as _np
    import concourse.bacc as _bacc
    from concourse.bass_utils import run_bass_kernel_spmd as _run

    nc = _bacc.Bacc("TRN2", target_bir_lowering=False, num_devices=1)
    arrays, dram = {}, {}
    for name, short in _INS.items():
        a = _np.ascontiguousarray(inputs[name])
        arrays[f"in_{name}_dram"] = a
        dram[short] = nc.dram_tensor(f"in_{name}_dram", a.shape, mybir.dt.from_np(a.dtype), kind="ExternalInput").ap()
    dram["out"] = nc.dram_tensor("out_0_dram", (B, T, D), fp32, kind="ExternalOutput").ap()
    build(nc, dram)
    r = _run(nc, [arrays], core_ids=[0])
    return r.results[0]["out_0_dram"]
```

```python
import concourse.bass as bass
from concourse import mybir
from contextlib import ExitStack

fp32 = mybir.dt.float32
f32r = mybir.dt.float32r
bf16 = mybir.dt.bfloat16
u32 = mybir.dt.uint32
ALU = mybir.AluOpType
ACT = mybir.ActivationFunctionType
AX = mybir.AxisListType

P = 128
B, T, D = 32, 256, 128
NTILE = B * T // P
LN_EPS = 1e-5
N_EPS = 1e-6
RMS_EPS = 1e-8
CAP = 10.0
SOFTPLUS_CUT = 30.0


class Count:

    def __init__(self, base, slope=0, i=None):
        self.base, self.slope, self.i = base, slope, i

    def __add__(self, n):
        return Count(self.base + n, self.slope, self.i)

    def __sub__(self, n):
        return self + -n

    def __mul__(self, n):
        return Count(self.base * n, self.slope * n, self.i)

    __rmul__ = __mul__

    def turn(self, buffers):
        return Count(self.base // buffers, self.slope // buffers, self.i)

    def of(self, buffers):
        return self.base % buffers

    def value(self):
        return self.base if self.i is None else self.i * self.slope + self.base

    def most(self, n):
        return Count(min(self.base, n)) if self.i is None else self

    def exists(self, count):
        return self.i is not None or 0 <= self.base < count


def need(engine, sem, count):
    if count.i is None and count.base <= 0:
        return
    assert count.base > 0
    engine.wait_ge(sem, count.value())


def need_apart(engine, met, *needs):
    needs = [(sem, count) for sem, count in needs if count.i is not None or count.base > 0]
    assert all(count.base > 0 for _, count in needs)
    values = [engine.to_reg(count.value()) if count.i is not None else count.base for _, count in needs]
    engine.wait_ge(*met)
    for (sem, _), value in zip(needs, values):
        engine.wait_ge(sem, value)


def steps(engine, count, lag, unroll, step, first):
    rounds = (count - first) // unroll
    for s in range(first):
        step(Count(s))
    with engine.Fori(0, rounds) as i:
        for k in range(unroll):
            step(Count(first + k, unroll, i))
    for s in range(first + rounds * unroll, count + lag):
        step(Count(s))


def recurrent_layer(nc, dram, const):
    GROUPS = NTILE // 4
    x_t = dram["x"].rearrange("b (h p) d -> p (b h) d", p=P)
    x1_t = dram["x1"].rearrange("(t p) d -> p t d", p=P)
    ident = const["ident"]
    ctx = ExitStack()
    with ctx:
        def sb(name, shape, dt=fp32):
            return ctx.enter_context(nc.sbuf_tensor(name, shape, dt))

        def sem(name):
            return ctx.enter_context(nc.semaphore(name))

        w_f = sb("a_w_f", [P, 4 * D])
        w_hi = sb("a_w_hi", [P, 4 * D], f32r)
        w_lo = sb("a_w_lo", [P, 4 * D], f32r)
        b_col = sb("a_b_col", [P, 4])
        ib_col = sb("a_ib_col", [P, 1])
        bias_i = sb("a_bias_i", [P, 1])
        bias_o = sb("a_bias_o", [P, 1])
        scale_b = sb("a_scale_b", [P, D])
        one_col = sb("a_one", [P, 1])
        eps_ln = sb("a_eps_ln", [P, 1])
        eps_n = sb("a_eps_n", [P, 1])
        eps_rms = sb("a_eps_rms", [P, 1])
        X = sb("a_X", [P, 3, 4, D])
        stats = sb("a_stats", [P, 2, 4, 6])
        mv = sb("a_mv", [P, 2, 4, 2])
        lnv = sb("a_lnv", [P, 2, 4])
        rstd = sb("a_rstd", [P, 2, 4])
        XN = sb("a_XN", [P, 2, 4, D])
        xt_hi = sb("a_xt_hi", [P, 2, 4 * P], f32r)
        xt_lo = sb("a_xt_lo", [P, 2, 4 * P], f32r)
        f_cut = sb("a_f_cut", [P, 512])
        f_exp = sb("a_f_exp", [P, 512])
        f_ln = sb("a_f_ln", [P, 512])
        sp = sb("a_sp", [P, 2, 512])
        i_tanh = sb("a_i_tanh", [P, 2, 512])
        i_neg = sb("a_i_neg", [P, 2, 512])
        z_tanh = sb("a_z_tanh", [P, 2, 512])
        o_tanh = sb("a_o_tanh", [P, 2, 512])
        M = sb("a_M", [P, 2, 2, T + 1])
        i_arg = sb("a_i_arg", [P, 512])
        f_sum = sb("a_f_sum", [P, 512])
        f_arg = sb("a_f_arg", [P, 512])
        i_s = sb("a_i_s", [P, 512])
        f_s = sb("a_f_s", [P, 512])
        iz = sb("a_iz", [P, 512])
        C = sb("a_C", [P, 512])
        N = sb("a_N", [P, 512])
        n_ln = sb("a_n_ln", [P, 512])
        n_inv = sb("a_n_inv", [P, 512])
        oc = sb("a_oc", [P, 512])
        H2 = sb("a_H2", [P, 2, 512])
        sq = sb("a_sq", [P, D])
        ss = sb("a_ss", [P, 4])
        ln_ss = sb("a_ln_ss", [P, 4])
        r_rms = sb("a_r_rms", [P, 4])
        Y = sb("a_Y", [P, 2, 4, D])
        X1 = sb("a_X1", [P, 2, 4, D])
        ps_t = ctx.enter_context(nc.psum_tensor("a_ps_t", [P, 2, 512], fp32))
        ps_g = ctx.enter_context(nc.psum_tensor("a_ps_g", [P, 4, 512], fp32))
        ps_h = ctx.enter_context(nc.psum_tensor("a_ps_h", [P, 2, 512], fp32))
        GI, GF, GO, GZ = range(4)

        s_load = sem("a_load")
        s_prep = sem("a_prep")
        s_whi = sem("a_whi")
        s_x = [sem(f"a_x{k}") for k in range(3)]
        s_mv = sem("a_mv_s")
        s_st = sem("a_st")
        s_lnv = sem("a_lnv_s")
        s_rstd = sem("a_rstd_s")
        s_xn = sem("a_xn_s")
        s_xt = sem("a_xt_s")
        s_xhi = sem("a_xhi")
        s_xlo = sem("a_xlo")
        s_g = sem("a_g")
        s_cut = sem("a_cut")
        s_fexp = sem("a_fexp")
        s_fln = sem("a_fln")
        s_sp = sem("a_sp_s")
        s_it = sem("a_it")
        s_in = sem("a_in")
        s_zt = sem("a_zt")
        s_ot = sem("a_ot")
        s_m = sem("a_m")
        s_ia = sem("a_ia")
        s_fsum = sem("a_fsum")
        s_fa = sem("a_fa")
        s_is = sem("a_is")
        s_fs = sem("a_fs")
        s_iz = sem("a_iz_s")
        s_cn = sem("a_cn")
        s_nln = sem("a_nln")
        s_ninv = sem("a_ninv")
        s_oc = sem("a_oc_s")
        s_h2 = sem("a_h2")
        s_ht = sem("a_ht")
        s_ss = sem("a_ss_s")
        s_lnss = sem("a_lnss")
        s_rms = sem("a_rms")
        s_y = sem("a_y")
        s_x1 = sem("a_x1_s")
        s_out = [sem(f"a_out{k}") for k in range(2)]
        block = ctx.enter_context(nc.Block())

        @block.sync
        def _(sync):
            sync.dma_start(w_f[:, :], dram["W"]).then_inc(s_load, 16)
            sync.dma_start(b_col[:, :], dram["b"].rearrange("(c p) -> p c", p=P), allow_slow_non_contiguous=True).then_inc(s_load, 16)
            sync.dma_start(ib_col[:, :], dram["input_bias"].rearrange("(p a) -> p a", a=1), allow_slow_non_contiguous=True).then_inc(s_load, 16)
            sync.dma_start(scale_b[:, :], dram["scale"].partition_broadcast(P)).then_inc(s_load, 16)

            sync.wait_ge(s_load, 64)

            def step(s):
                if (s - 0).exists(GROUPS):
                    need_apart(sync, (s_load, 64), (s_x1, s - 2))
                    sync.dma_start(X[:, s.of(3)], x_t[:, bass.ds((s * 4).value(), 4), :]).then_inc(s_x[s.of(3)], 16)
                if (s - 3).exists(GROUPS):
                    g = s - 3
                    need_apart(sync, (s_load, 64), (s_x1, g + 1))
                    sync.dma_start(x1_t[:, bass.ds((g * 4).value(), 4), :], X1[:, g.of(2)]).then_inc(s_out[g.of(2)], 16)

            steps(sync, GROUPS, 3, 6, step, 6)
            for k in range(2):
                sync.wait_ge(s_out[k], 16 * GROUPS // 2)

        @block.gpsimd
        def _(pool):
            def step(s):
                if (s - 1).exists(GROUPS):
                    g = s - 1
                    j = g.of(2)
                    need(pool, s_it, g + 1)
                    need(pool, s_ia, g - 1)
                    nc.gpsimd.tensor_scalar(i_neg[:, j], i_tanh[:, j], CAP, None, ALU.mult).then_inc(s_in, 1)
                    need(pool, s_m, g + 1)
                    need(pool, s_fa, g)
                    nc.gpsimd.tensor_tensor(f_sum[:, :].rearrange("p (b t) -> p b t", b=2), M[:, j, :, 0:T],
                                            sp[:, j].rearrange("p (b t) -> p b t", b=2), ALU.add).then_inc(s_fsum, 1)
                    need(pool, s_fsum, g + 1)
                    need(pool, s_fs, g)
                    nc.gpsimd.tensor_tensor(f_arg[:, :].rearrange("p (b t) -> p b t", b=2), M[:, j, :, 1:T + 1],
                                            f_sum[:, :].rearrange("p (b t) -> p b t", b=2), ALU.subtract).then_inc(s_fa, 1)
                if (s - 2).exists(GROUPS):
                    g = s - 2
                    j = g.of(2)
                    need(pool, s_y, g + 1)
                    need(pool, s_out[j], g.turn(2) * 16)
                    nc.gpsimd.tensor_tensor(X1[:, j], Y[:, j], X[:, g.of(3)], ALU.add).then_inc(s_x1, 1)

            steps(pool, GROUPS, 2, 6, step, 6)

        @block.scalar
        def _(act):
            act.wait_ge(s_load, 64)
            act.wait_ge(s_prep, 5)
            nc.scalar.copy(w_hi[:, :], w_f[:, :]).then_inc(s_whi, 1)

            def step(s):
                j = (s - 1).of(2)
                if (s - 1).exists(GROUPS):
                    g = s - 1
                    need(act, s_g, 4 * g + 1 + GI)
                    need(act, s_in, g - 1)
                    nc.scalar.activation(i_tanh[:, j], ps_g[:, GI], ACT.Tanh, bias=bias_i[:, :], scale=-1.0 / CAP).then_inc(s_it, 1)
                    need(act, s_g, 4 * g + 1 + GO)
                    need(act, s_oc, g - 1)
                    nc.scalar.activation(o_tanh[:, j], ps_g[:, GO], ACT.Tanh, bias=bias_o[:, :], scale=0.5).then_inc(s_ot, 1)
                    need(act, s_g, 4 * g + 1 + GZ)
                    need(act, s_iz, g - 1)
                    nc.scalar.activation(z_tanh[:, j], ps_g[:, GZ], ACT.Tanh, bias=b_col[:, GZ:GZ + 1]).then_inc(s_zt, 1)
                if (s - 0).exists(GROUPS):
                    g, j0 = s, s.of(2)
                    need(act, s_mv, g + 1)
                    need(act, s_rstd, g - 1)
                    nc.scalar.activation(lnv[:, j0], mv[:, j0, :, 1], ACT.Ln, bias=eps_ln[:, :]).then_inc(s_lnv, 1)
                    need(act, s_lnv, g + 1)
                    need(act, s_xn, g - 1)
                    nc.scalar.activation(rstd[:, j0], lnv[:, j0], ACT.Exp, scale=-0.5).then_inc(s_rstd, 1)
                if (s - 1).exists(GROUPS):
                    g = s - 1
                    need(act, s_cut, g + 1)
                    need(act, s_fln, g)
                    nc.scalar.activation(f_exp[:, :], f_cut[:, :], ACT.Exp).then_inc(s_fexp, 1)
                    need(act, s_fexp, g + 1)
                    need(act, s_sp, g)
                    nc.scalar.activation(f_ln[:, :], f_exp[:, :], ACT.Ln, bias=one_col[:, :]).then_inc(s_fln, 1)
                if (s - 2).exists(GROUPS):
                    g, j0 = s - 2, s.of(2)
                    need(act, s_ht, g + 1)
                    need(act, s_lnss, g)
                    for t in range(4):
                        need(act, s_ss, 4 * g + t)
                        nc.scalar.activation(sq[:, :], ps_h[:, j0, t * P:(t + 1) * P], ACT.Square,
                                             accum_out=ss[:, t:t + 1]).then_inc(s_ss, 1)
                    need(act, s_ss, 4 * g + 4)
                    nc.scalar.activation(ln_ss[:, :], ss[:, :], ACT.Ln, bias=eps_rms[:, :], scale=1.0 / D).then_inc(s_lnss, 1)
                    need(act, s_lnss, g + 1)
                    need(act, s_y, g)
                    nc.scalar.activation(r_rms[:, :], ln_ss[:, :], ACT.Exp, scale=-0.5).then_inc(s_rms, 1)
                if (s - 0).exists(GROUPS):
                    g, j0 = s, s.of(2)
                    need(act, s_xt, g + 1)
                    need(act, s_g, 4 * (g - 1))
                    nc.scalar.copy(xt_hi[:, j0], ps_t[:, j0]).then_inc(s_xhi, 1)
                if (s - 1).exists(GROUPS):
                    g = s - 1
                    need(act, s_ia, g + 1)
                    need(act, s_cn, 2 * g)
                    nc.scalar.activation(i_s[:, :], i_arg[:, :], ACT.Exp).then_inc(s_is, 1)
                    need(act, s_fa, g + 1)
                    nc.scalar.activation(f_s[:, :], f_arg[:, :], ACT.Exp).then_inc(s_fs, 1)
                    need(act, s_cn, 2 * g + 1)
                    need(act, s_ninv, g)
                    nc.scalar.activation(n_ln[:, :], N[:, :], ACT.Ln, bias=eps_n[:, :]).then_inc(s_nln, 1)
                    need(act, s_nln, g + 1)
                    need(act, s_h2, g)
                    nc.scalar.activation(n_inv[:, :], n_ln[:, :], ACT.Exp, scale=-1.0).then_inc(s_ninv, 1)

            steps(act, GROUPS, 2, 6, step, 6)

        @block.vector
        def _(dve):
            nc.vector.memset(one_col[:, :], 1.0)
            nc.vector.memset(eps_ln[:, :], LN_EPS)
            nc.vector.memset(eps_n[:, :], N_EPS)
            nc.vector.memset(eps_rms[:, :], 4 * RMS_EPS).then_inc(s_prep, 1)
            nc.vector.memset(M[:, :, :, 0:1], 0.0).then_inc(s_prep, 1)
            dve.wait_ge(s_load, 64)
            nc.vector.tensor_tensor(bias_i[:, :], b_col[:, GI:GI + 1], ib_col[:, :], ALU.add).then_inc(s_prep, 1)
            dve.wait_ge(s_prep, 3)
            nc.vector.tensor_scalar(bias_i[:, :], bias_i[:, :], -1.0 / CAP, None, ALU.mult).then_inc(s_prep, 1)
            nc.vector.tensor_scalar(bias_o[:, :], b_col[:, GO:GO + 1], 0.5, None, ALU.mult).then_inc(s_prep, 1)
            dve.wait_ge(s_whi, 1)
            nc.vector.tensor_tensor(w_lo[:, :], w_f[:, :], w_hi[:, :].bitcast(fp32), ALU.subtract).then_inc(s_prep, 1)

            def step(s):
                j, j0 = (s - 1).of(2), s.of(2)
                if (s - 1).exists(GROUPS):
                    g = s - 1
                    need(dve, s_g, 4 * g + 1 + GF)
                    need(dve, s_fexp, g)
                    nc.vector.tensor_scalar(f_cut[:, :], ps_g[:, GF], b_col[:, GF:GF + 1], SOFTPLUS_CUT,
                                            ALU.add, ALU.min).then_inc(s_cut, 1)
                if (s - 0).exists(GROUPS):
                    g = s
                    need(dve, s_x[s.of(3)], g.turn(3) * 16 + 16)
                    for t in range(4):
                        last = nc.vector.bn_stats(stats[:, j0, t, :], X[:, s.of(3), t, :])
                    last.then_inc(s_st, 1)
                    need_apart(dve, (s_prep, 1), (s_st, g + 1), (s_lnv, g - 1))
                    for t in range(4):
                        last = nc.vector.bn_aggr(mv[:, j0, t, :], stats[:, j0, t, :])
                    last.then_inc(s_mv, 1)
                if (s - 1).exists(GROUPS):
                    g = s - 1
                    need(dve, s_fln, g + 1)
                    nc.vector.scalar_tensor_tensor(out=sp[:, j], in0=ps_g[:, GF], scalar=b_col[:, GF:GF + 1],
                                                   in1=f_ln[:, :], op0=ALU.add, op1=ALU.max).then_inc(s_sp, 1)
                    need(dve, s_sp, g + 1)
                    need(dve, s_in, g + 1)
                    for b in range(2):
                        last = nc.vector.tensor_tensor_scan(M[:, j, b, 1:T + 1], sp[:, j, b * T:(b + 1) * T],
                                                            i_neg[:, j, b * T:(b + 1) * T], 0.0, ALU.add, ALU.min)
                    last.then_inc(s_m, 1)
                    need(dve, s_m, g + 1)
                    need(dve, s_is, g)
                    nc.vector.tensor_tensor(i_arg[:, :].rearrange("p (b t) -> p b t", b=2), M[:, j, :, 1:T + 1],
                                            i_neg[:, j].rearrange("p (b t) -> p b t", b=2), ALU.subtract).then_inc(s_ia, 1)
                if (s - 0).exists(GROUPS):
                    g = s
                    need(dve, s_rstd, g + 1)
                    need(dve, s_xt, g - 1)
                    for t in range(4):
                        last = nc.vector.tensor_scalar(XN[:, j0, t, :], X[:, s.of(3), t, :], mv[:, j0, t, 0:1],
                                                       rstd[:, j0, t:t + 1], ALU.subtract, ALU.mult)
                    last.then_inc(s_xn, 1)
                if (s - 2).exists(GROUPS):
                    g = s - 2
                    need(dve, s_rms, g + 1)
                    need(dve, s_x1, g - 1)
                    for t in range(4):
                        last = nc.vector.scalar_tensor_tensor(out=Y[:, j0, t, :], in0=ps_h[:, j0, t * P:(t + 1) * P],
                                                              scalar=r_rms[:, t:t + 1], in1=scale_b[:, :],
                                                              op0=ALU.mult, op1=ALU.mult)
                    last.then_inc(s_y, 1)
                if (s - 0).exists(GROUPS):
                    g = s
                    need(dve, s_xhi, g + 1)
                    nc.vector.tensor_tensor(xt_lo[:, j0], ps_t[:, j0], xt_hi[:, j0].bitcast(fp32), ALU.subtract).then_inc(s_xlo, 1)
                if (s - 1).exists(GROUPS):
                    g = s - 1
                    need(dve, s_is, g + 1)
                    need(dve, s_zt, g + 1)
                    nc.vector.tensor_tensor(iz[:, :], i_s[:, :], z_tanh[:, j], ALU.mult).then_inc(s_iz, 1)
                    need(dve, s_fs, g + 1)
                    need(dve, s_nln, g)
                    for b in range(2):
                        q = slice(b * T, (b + 1) * T)
                        last = nc.vector.tensor_tensor_scan(N[:, q], f_s[:, q], i_s[:, q], 0.0, ALU.mult, ALU.add)
                    last.then_inc(s_cn, 1)
                    need(dve, s_iz, g + 1)
                    for b in range(2):
                        q = slice(b * T, (b + 1) * T)
                        last = nc.vector.tensor_tensor_scan(C[:, q], f_s[:, q], iz[:, q], 0.0, ALU.mult, ALU.add)
                    last.then_inc(s_cn, 1)
                    need(dve, s_cn, 2 * g + 2)
                    need(dve, s_ot, g + 1)
                    nc.vector.scalar_tensor_tensor(out=oc[:, :], in0=o_tanh[:, j], scalar=1.0, in1=C[:, :],
                                                   op0=ALU.add, op1=ALU.mult).then_inc(s_oc, 1)
                    need(dve, s_oc, g + 1)
                    need(dve, s_ninv, g + 1)
                    need(dve, s_ht, g - 1)
                    nc.vector.tensor_tensor(H2[:, j], oc[:, :], n_inv[:, :], ALU.mult).then_inc(s_h2, 1)

            steps(dve, GROUPS, 2, 6, step, 6)

        @block.tensor
        def _(pe):
            pe.wait_ge(s_prep, 6)

            def step(s):
                j, j0 = (s - 1).of(2), s.of(2)
                if (s - 0).exists(GROUPS):
                    g = s
                    need(pe, s_xn, g + 1)
                    need(pe, s_xlo, g - 1)
                    for t in range(4):
                        last = nc.tensor.transpose(ps_t[:, j0, t * P:(t + 1) * P], XN[:, j0, t, :], ident[:, :])
                    last.then_inc(s_xt, 1)
                if (s - 1).exists(GROUPS):
                    g = s - 1
                    need(pe, s_h2, g + 1)
                    need(pe, s_y, g - 1)
                    for t in range(4):
                        last = nc.tensor.transpose(ps_h[:, j, t * P:(t + 1) * P], H2[:, j, t * P:(t + 1) * P], ident[:, :])
                    last.then_inc(s_ht, 1)
                if (s - 0).exists(GROUPS):
                    g = s
                    need(pe, s_xlo, g + 1)
                    for c, freed in ((GI, s_it), (GF, s_sp), (GO, s_ot), (GZ, s_zt)):
                        need(pe, freed, g)
                        w = slice(c * D, (c + 1) * D)
                        nc.tensor.matmul(ps_g[:, c], w_lo[:, w], xt_hi[:, j0], start=True, stop=False)
                        nc.tensor.matmul(ps_g[:, c], w_hi[:, w], xt_lo[:, j0], start=False, stop=False)
                        nc.tensor.matmul(ps_g[:, c], w_hi[:, w], xt_hi[:, j0], start=False, stop=True).then_inc(s_g, 1)

            steps(pe, GROUPS, 2, 6, step, 6)

HEADS, HD = 16, 8
NG, NJ = 4, 4
PARTS = 3
ROWS = PARTS * HD
M_ROW = ROWS
VW = 32
NEG = -1e30
NB = 5


def attention(nc, dram, const):
    x1_t = dram["x1"].rearrange("(b t p) d -> b p t d", p=P, t=2)
    h_t = dram["h"].rearrange("(b t p) d -> b p t d", p=P, t=2)
    scr = dram["qk_scr"]
    ident, ident_b, mask_b = const["ident"], const["ident_b"], const["mask_b"]
    ctx = ExitStack()
    with ctx:
        def sb(name, shape, dt=fp32):
            return ctx.enter_context(nc.sbuf_tensor(name, shape, dt))

        def sem(name):
            return ctx.enter_context(nc.semaphore(name))

        w_f = sb("b_w_f", [P, 3 * D])
        w_hi = sb("b_w_hi", [P, 3 * D], f32r)
        w_lo = sb("b_w_lo", [P, 3 * D], f32r)
        wo = sb("b_wo", [P, D])
        g_b = sb("b_g", [P, 1, D])
        b_b = sb("b_b", [P, 1, D])
        eps_ln = sb("b_eps", [P, 1])
        zero_row = sb("b_zero", [HEADS, T])
        X = sb("b_X", [P, NB, 2, D])
        stats = sb("b_stats", [P, 2, 6])
        mv = sb("b_mv", [P, 2, 2])
        lnv = sb("b_lnv", [P, 2])
        rstd = sb("b_rstd", [P, 2])
        XN = sb("b_XN", [P, NB, 2, D])
        xt_hi = sb("b_xt_hi", [P, T], f32r)
        xt_lo = sb("b_xt_lo", [P, T], f32r)
        qk_hi = sb("b_qk_hi", [P, 2, T], f32r)
        qk_lo = sb("b_qk_lo", [P, 2, T], f32r)
        V = sb("b_V", [P, NB, 2, HEADS, VW])
        QK = sb("b_QK", [P, NB, NJ + 1, NG, T], f32r)
        m_neg = sb("b_m_neg", [P, NB, 2, HEADS])
        mt = sb("b_mt", [HEADS, T], f32r)
        PT = sb("b_PT", [P, 2, 3, 512])
        OT = sb("b_OT", [P, 2, T])
        rec = sb("b_rec", [P, 2, NJ])
        attn = sb("b_attn", [P, NB, 2, NG, NJ, HD])
        at = sb("b_at", [P, T])
        R = sb("b_R", [P, 2, D])
        stats1 = sb("b_stats1", [P, 2, 6])
        mv1 = sb("b_mv1", [P, 2, 2])
        lnv1 = sb("b_lnv1", [P, 2])
        rstd1 = sb("b_rstd1", [P, 2])
        H0 = sb("b_H0", [P, 2, D])
        H1 = sb("b_H1", [P, 2, D])
        H = sb("b_H", [P, NB, 2, D])
        ps_s = ctx.enter_context(nc.psum_tensor("b_ps_s", [P, 3, 512], fp32))
        ps_m = ctx.enter_context(nc.psum_tensor("b_ps_m", [P, 2, 512], fp32))
        ps_o = ctx.enter_context(nc.psum_tensor("b_ps_o", [P, 2, T], fp32))
        ps_x = ctx.enter_context(nc.psum_tensor("b_ps_x", [P, 2, 512], fp32))

        s_load = sem("b_load")
        s_whi = sem("b_whi")
        s_prep = sem("b_prep")
        s_fill = sem("b_fill")
        s_x = [sem(f"b_x{k}") for k in range(NB)]
        s_st = sem("b_st")
        s_mv = sem("b_mvs")
        s_lnv = sem("b_lnvs")
        s_rstd = sem("b_rstds")
        s_xn = sem("b_xn")
        s_xt = sem("b_xt")
        s_xhi = sem("b_xhi")
        s_xlo = sem("b_xlo")
        s_qk = sem("b_qk")
        s_qkhi = sem("b_qkhi")
        s_qklo = sem("b_qklo")
        s_v = sem("b_v")
        s_vc = sem("b_vc")
        s_qkw = [sem(f"b_qkw{k}") for k in range(NB)]
        s_qkr = [sem(f"b_qkr{k}") for k in range(NB)]
        s_b = sem("b_b_s")
        s_red = sem("b_red")
        s_mt = sem("b_mts")
        s_mtc = sem("b_mtc")
        s_mr = [sem(f"b_mr{k}") for k in range(NB)]
        s_s = sem("b_s")
        s_e = sem("b_e")
        s_k = sem("b_k")
        s_pv = sem("b_pv")
        s_ot = sem("b_ot")
        s_ott = sem("b_ott")
        s_rec = sem("b_recs")
        s_att = sem("b_att")
        s_aT = sem("b_aT")
        s_at = sem("b_ats")
        s_wo = sem("b_wos")
        s_r = sem("b_r")
        s_st1 = sem("b_st1")
        s_mv1 = sem("b_mv1s")
        s_lnv1 = sem("b_lnv1s")
        s_rstd1 = sem("b_rstd1s")
        s_h0 = sem("b_h0")
        s_h1 = sem("b_h1")
        s_h = sem("b_h")
        s_out = [sem(f"b_out{k}") for k in range(NB)]
        block = ctx.enter_context(nc.Block())
        OB = [1, 1, 0, 0]
        WRITES, READS = 3 * 16, 5 * 16

        def by_head(w, c, j):
            return w[:, c * D:(c + 1) * D].rearrange("p (g j r) -> p j r g", g=NG, j=NJ)[:, j]

        def by_dim(w, c, j):
            return w[:, c * D:(c + 1) * D].rearrange("p (r j g) -> p j r g", g=NG, j=NJ)[:, j]

        @block.sync
        def _(sync):
            sync.dma_start(w_f[:, :], dram["w_qkv"]).then_inc(s_load, 16)
            sync.dma_start(wo[:, :], dram["w_o"]).then_inc(s_load, 16)
            sync.dma_start(g_b[:, 0, :], dram["g1"].partition_broadcast(P)).then_inc(s_load, 16)
            sync.dma_start(b_b[:, 0, :], dram["b1"].partition_broadcast(P)).then_inc(s_load, 16)
            sync.wait_ge(s_fill, 4)

            def step(s):
                if s.exists(B):
                    b, n = s, s.of(NB)
                    need_apart(sync, (s_fill, 4), (s_xn, b - (NB - 1)))
                    sync.dma_start(X[:, n], x1_t[bass.ds(b.value(), 1)].rearrange("b p t d -> p (b t) d")).then_inc(s_x[n], 16)
                if (s - 3).exists(B):
                    b, n = s - 3, (s - 3).of(NB)
                    need(sync, s_mtc, b + 1)
                    sync.dma_start(QK[M_ROW:M_ROW + 1, n, 0:NJ].rearrange("o j g n -> o (j g) n").bitcast(fp32), mt[:, :].bitcast(fp32)).then_inc(s_mr[n], 16)
                if (s - 1).exists(B):
                    b, n = s - 1, (s - 1).of(NB)
                    need_apart(sync, (s_fill, 4), (s_qkhi, b + 1), (s_qkr[n], b.turn(NB) * READS))
                    slots = scr[n].rearrange("s p n -> p s n")
                    sync.dma_start(slots[:, 0:4:3], qk_hi[:, :, :].bitcast(fp32)).then_inc(s_qkw[n], 16)
                    sync.dma_start(slots[:, 1:6:4], qk_hi[:, :, :].bitcast(fp32)).then_inc(s_qkw[n], 16)
                    need(sync, s_qklo, b + 1)
                    sync.dma_start(slots[:, 2:5:2], qk_lo[:, :, :].bitcast(fp32)).then_inc(s_qkw[n], 16)
                    need(sync, s_s, (b - NB) * 12 + 12)
                    sync.dma_start(QK[M_ROW:M_ROW + 1, n, 0:NJ].rearrange("o j g n -> o (j g) n").bitcast(fp32), zero_row[:, :]).then_inc(s_qkr[n], 16)
                if (s - 6).exists(B):
                    b, n = s - 6, (s - 6).of(NB)
                    need_apart(sync, (s_fill, 4), (s_h, b + 1))
                    sync.dma_start(h_t[bass.ds(b.value(), 1)].rearrange("b p t d -> p (b t) d"), H[:, n]).then_inc(s_out[n], 16)
                if (s - 1).exists(B):
                    b, n = s - 1, (s - 1).of(NB)
                    need(sync, s_qkw[n], b.turn(NB) * WRITES + WRITES)
                    rows = scr[n].rearrange("(a s) (r j g) n -> j (s r) a (g n)", a=2, g=NG, j=NJ)
                    for j in range(NJ):
                        sync.dma_start(QK[32 * j:32 * j + ROWS, n, j:NJ + 1:NJ - j].rearrange("p a g n -> p a (g n)").bitcast(fp32), rows[j]).then_inc(s_qkr[n], 16)

            sync.wait_ge(s_load, 64)
            steps(sync, B, 6, NB, step, 12)
            for k in range(NB):
                sync.wait_ge(s_out[k], 16 * len(range(k, B, NB)))

        @block.gpsimd
        def _(pool):
            nc.gpsimd.memset(zero_row[:, :], 0.0).then_inc(s_fill, 1)
            nc.gpsimd.memset(QK[:, :, 0:NJ].bitcast(fp32), 0.0)
            nc.gpsimd.memset(V[:, :, :, :, :], 0.0).then_inc(s_fill, 1)
            pool.wait_ge(s_fill, 2)
            nc.gpsimd.memset(V[:, :, :, :, HD:HD + 1], 1.0).then_inc(s_fill, 1)
            nc.gpsimd.memset(QK[:, :, NJ].bitcast(fp32), 1.0).then_inc(s_fill, 1)
            pool.wait_ge(s_fill, 4)

            def mask(b, g):
                for u in range(3):
                    need_apart(pool, (s_fill, 4), (s_e, 12 * b + (3 * g + u + 1)))
                    if u == 0:
                        tri = PT[:, g % 2, u].rearrange("p (j q) -> p j q", j=NJ)
                    else:
                        tri = PT[:, g % 2, u].rearrange("p (j q) -> p j q", j=2)[:, :, 0:P]
                    nc.gpsimd.affine_select(out=tri, in_=tri, compare_op=ALU.is_ge, fill=0.0, base=0,
                                            pattern=[[0, tri.shape[1]], [1, P]], channel_multiplier=-1).then_inc(s_k, 1)

            def step(s):
                c, d = s - 4, s - 6
                for g in range(NG):
                    if c.exists(B):
                        mask(c, g)
                    if g == 0 and d.exists(B):
                        n = d.of(NB)
                        need(pool, s_h0, d + 1)
                        need(pool, s_h, d)
                        nc.gpsimd.tensor_tensor(H1[:, :, :], H0[:, :, :], g_b[:, :, :].to_broadcast([P, 2, D]), ALU.mult).then_inc(s_h1, 1)
                        need(pool, s_h1, d + 1)
                        need(pool, s_out[n], d.turn(NB) * 16)
                        nc.gpsimd.tensor_tensor(H[:, n], H1[:, :, :], b_b[:, :, :].to_broadcast([P, 2, D]), ALU.add).then_inc(s_h, 1)

            steps(pool, B, 6, NB, step, 12)

        @block.scalar
        def _(act):
            act.preload_act_table_set("natural_log_exp_and_others")
            act.wait_ge(s_load, 64)
            for c in range(2):
                for j in range(NJ):
                    nc.scalar.copy(by_dim(w_hi, c, j), by_head(w_f, c, j))
            nc.scalar.copy(w_hi[:, 2 * D:], w_f[:, 2 * D:]).then_inc(s_whi, 1)
            act.wait_ge(s_fill, 4)
            act.wait_ge(s_prep, 1)

            def exps(b, g):
                for u in range(3):
                    need(act, s_s, 12 * b + (3 * g + u + 1))
                    need(act, s_pv, 4 * b + (g - 1))
                    nc.scalar.activation(PT[:, g % 2, u], ps_s[:, u], ACT.Exp, scale=HD ** -0.5).then_inc(s_e, 1)

            def evac_o(b, g):
                need(act, s_pv, 4 * b + (g + 1))
                need(act, s_ott, 4 * b + (g - 1))
                nc.scalar.copy(OT[:, g % 2], ps_o[:, g % 2]).then_inc(s_ot, 1)

            def step(s):
                n, a, b1, c, p, q = s, s - 1, s - 3, s - 4, s - 5, s - 6
                if c.exists(B):
                    exps(c, 0)
                if q.exists(B):
                    need(act, s_mv1, q + 1)
                    need(act, s_rstd1, q)
                    nc.scalar.activation(lnv1[:, :], mv1[:, :, 1], ACT.Ln, bias=eps_ln[:, :]).then_inc(s_lnv1, 1)
                    need(act, s_lnv1, q + 1)
                    need(act, s_h0, q)
                    nc.scalar.activation(rstd1[:, :], lnv1[:, :], ACT.Exp, scale=-0.5).then_inc(s_rstd1, 1)
                if p.exists(B):
                    evac_o(p, 3)
                if a.exists(B):
                    need(act, s_xt, a + 1)
                    need(act, s_v, a)
                    nc.scalar.copy(xt_hi[:, :], ps_x[:, 1, 0:T]).then_inc(s_xhi, 1)
                if c.exists(B):
                    exps(c, 1)
                if b1.exists(B):
                    need(act, s_mt, b1 + 1)
                    need(act, s_mr[(b1 - 1).of(NB)], (b1 - 1).turn(NB) * 16 + 16)
                    nc.scalar.copy(mt[:, :], ps_x[0:HEADS, 0, 0:T]).then_inc(s_mtc, 1)
                if c.exists(B):
                    evac_o(c, 0)
                if a.exists(B):
                    need(act, s_qk, a + 1)
                    need(act, s_qkw[(a - 1).of(NB)], (a - 1).turn(NB) * WRITES + WRITES)
                    need(act, s_qklo, a)
                    nc.scalar.copy(qk_hi[:, :, :].rearrange("p a n -> p (a n)"), ps_x[:, 1]).then_inc(s_qkhi, 1)
                if c.exists(B):
                    exps(c, 2)
                if p.exists(B):
                    need(act, s_aT, p + 1)
                    need(act, s_wo, p)
                    nc.scalar.copy(at[:, :], ps_x[:, 0, 0:T]).then_inc(s_at, 1)
                if c.exists(B):
                    evac_o(c, 1)
                if a.exists(B):
                    need(act, s_v, a + 1)
                    need(act, s_pv, 4 * (a - NB) + 4)
                    nc.scalar.copy(V[:, a.of(NB), :, :, 0:HD], ps_x[:, 1, 0:T].rearrange("p (t h r) -> p t h r", t=2, h=HEADS)).then_inc(s_vc, 1)
                if n.exists(B):
                    need(act, s_mv, n + 1)
                    need(act, s_rstd, n)
                    nc.scalar.activation(lnv[:, :], mv[:, :, 1], ACT.Ln, bias=eps_ln[:, :]).then_inc(s_lnv, 1)
                    need(act, s_lnv, n + 1)
                    need(act, s_xn, n)
                    nc.scalar.activation(rstd[:, :], lnv[:, :], ACT.Exp, scale=-0.5).then_inc(s_rstd, 1)
                if c.exists(B):
                    exps(c, 3)
                if c.exists(B):
                    evac_o(c, 2)

            steps(act, B, 6, NB, step, 12)

        @block.vector
        def _(dve):
            nc.vector.memset(eps_ln[:, :], LN_EPS).then_inc(s_prep, 1)
            dve.wait_ge(s_whi, 1)
            for c in range(2):
                for j in range(NJ):
                    nc.vector.tensor_tensor(by_dim(w_lo, c, j), by_head(w_f, c, j), by_dim(w_hi, c, j).bitcast(fp32), ALU.subtract)
            nc.vector.tensor_tensor(w_lo[:, 2 * D:], w_f[:, 2 * D:], w_hi[:, 2 * D:].bitcast(fp32), ALU.subtract).then_inc(s_prep, 1)

            def reduces(b, first, last):
                for u in range(first, last):
                    need(dve, s_b, 12 * b + (u + 1))
                    need(dve, s_mt, b - (NB - 1))
                    if u < 4:
                        scores, out = ps_m[:, u % 2].rearrange("p (j k) -> p j k", j=4), m_neg[:, b.of(NB), 0, u::NG]
                    else:
                        g, jp = divmod(u - 4, 2)
                        scores, out = ps_m[:, u % 2].rearrange("p (j k) -> p j k", j=2), m_neg[:, b.of(NB), 1, 8 * jp + g:8 * jp + g + 5:NG]
                    nc.vector.tensor_reduce(out, scores, AX.X, ALU.max, negate=True).then_inc(s_red, 1)

            def norm_o(b, g):
                need(dve, s_ott, 4 * b + (g + 1))
                need(dve, s_att, 4 * b + g)
                o = ps_x[:, OB[g], 0:T].rearrange("p (t j r) -> p t j r", t=2, j=NJ)
                nc.vector.reciprocal(rec[:, :, :], o[:, :, :, HD]).then_inc(s_rec, 1)
                need(dve, s_rec, 4 * b + (g + 1))
                need(dve, s_aT, b - 1)
                nc.vector.tensor_tensor(attn[:, b.of(NB), :, g], o[:, :, :, 0:HD],
                                        rec[:, :, :].unsqueeze(3).to_broadcast([P, 2, NJ, HD]), ALU.mult).then_inc(s_att, 1)

            def step(s):
                n, a, b, b1, c, p, q = s, s - 1, s - 2, s - 3, s - 4, s - 5, s - 6
                if b1.exists(B):
                    reduces(b1, 9, 11)
                if a.exists(B):
                    k = a.of(NB)
                    need(dve, s_rstd, a + 1)
                    for t in range(2):
                        last = nc.vector.tensor_scalar(XN[:, k, t, :], X[:, k, t, :], mv[:, t, 0:1],
                                                       rstd[:, t:t + 1], ALU.subtract, ALU.mult)
                    last.then_inc(s_xn, 1)
                if b1.exists(B):
                    reduces(b1, 11, 12)
                if p.exists(B):
                    norm_o(p, 2)
                if q.exists(B):
                    need(dve, s_rstd1, q + 1)
                    need(dve, s_h1, q)
                    for t in range(2):
                        last = nc.vector.tensor_scalar(H0[:, t, :], R[:, t, :], mv1[:, t, 0:1],
                                                       rstd1[:, t:t + 1], ALU.subtract, ALU.mult)
                    last.then_inc(s_h0, 1)
                if b.exists(B):
                    reduces(b, 0, 1)
                if a.exists(B):
                    need(dve, s_xhi, a + 1)
                    nc.vector.tensor_tensor(xt_lo[:, :], ps_x[:, 1, 0:T], xt_hi[:, :].bitcast(fp32), ALU.subtract).then_inc(s_xlo, 1)
                if b.exists(B):
                    reduces(b, 1, 4)
                if a.exists(B):
                    need(dve, s_qkhi, a + 1)
                    need(dve, s_qkw[(a - 1).of(NB)], (a - 1).turn(NB) * WRITES + WRITES)
                    nc.vector.tensor_tensor(qk_lo[:, :, :].rearrange("p a n -> p (a n)"), ps_x[:, 1],
                                            qk_hi[:, :, :].bitcast(fp32).rearrange("p a n -> p (a n)"), ALU.subtract).then_inc(s_qklo, 1)
                if p.exists(B):
                    norm_o(p, 3)
                if b.exists(B):
                    reduces(b, 4, 6)
                if c.exists(B):
                    norm_o(c, 0)
                if n.exists(B):
                    k = n.of(NB)
                    need(dve, s_x[k], n.turn(NB) * 16 + 16)
                    need(dve, s_mv, n)
                    for t in range(2):
                        last = nc.vector.bn_stats(stats[:, t, :], X[:, k, t, :])
                    last.then_inc(s_st, 1)
                    need_apart(dve, (s_prep, 1), (s_st, n + 1))
                    for t in range(2):
                        last = nc.vector.bn_aggr(mv[:, t, :], stats[:, t, :])
                    last.then_inc(s_mv, 1)
                if b.exists(B):
                    reduces(b, 6, 8)
                if p.exists(B):
                    need(dve, s_wo, p + 1)
                    need(dve, s_h0, p)
                    nc.vector.tensor_tensor(R[:, :, :], ps_x[:, 0, 0:T].rearrange("p (t d) -> p t d", t=2), XN[:, p.of(NB)], ALU.add).then_inc(s_r, 1)
                    need(dve, s_r, p + 1)
                    for t in range(2):
                        last = nc.vector.bn_stats(stats1[:, t, :], R[:, t, :])
                    last.then_inc(s_st1, 1)
                    need_apart(dve, (s_prep, 1), (s_st1, p + 1), (s_lnv1, p))
                    for t in range(2):
                        last = nc.vector.bn_aggr(mv1[:, t, :], stats1[:, t, :])
                    last.then_inc(s_mv1, 1)
                if b.exists(B):
                    reduces(b, 8, 9)
                if c.exists(B):
                    norm_o(c, 1)

            steps(dve, B, 6, NB, step, 12)

        @block.tensor
        def _(pe):
            pe.wait_ge(s_prep, 2)

            def scores(c, g):
                n = c.of(NB)
                if g == 0:
                    need(pe, s_mr[n], c.turn(NB) * 16 + 16)
                need(pe, s_e, 12 * c + (3 * g - 2))
                nc.tensor.matmul(ps_s[:, 0].rearrange("p (j q) -> p j q", j=NJ), QK[:, n, NJ, g, P:T], QK[:, n, 0:NJ, g, P:T],
                                 start=True, stop=True).then_inc(s_s, 1)
                for u in (1, 2):
                    need(pe, s_e, 12 * c + (3 * g - 2 + u))
                    nc.tensor.matmul(ps_s[:, u].rearrange("p (j q) -> p j q", j=2), QK[:, n, NJ, g, 0:P], QK[:, n, 2 * u - 2:2 * u, g, :],
                                     start=True, stop=True).then_inc(s_s, 1)

            def maxima(b, first, last):
                n = b.of(NB)
                if first == 0:
                    need(pe, s_qkr[n], b.turn(NB) * READS + READS)
                for u in range(first, last):
                    need(pe, s_red, 12 * b + (u - 1))
                    if u < 4:
                        nc.tensor.matmul(ps_m[:, u % 2].rearrange("p (j k) -> p j k", j=4), ident_b[:, :], mask_b[:, :, :],
                                         start=True, stop=False, skip_group_check=True)
                        for j in range(4):
                            done = nc.tensor.matmul(ps_m[:, u % 2, j * P:(j + 1) * P], QK[:, n, j, u, 0:P], QK[:, n, NJ, u, 0:P],
                                                    start=False, stop=(j == 3), skip_group_check=True)
                    else:
                        g, jp = divmod(u - 4, 2)
                        nc.tensor.matmul(ps_m[:, u % 2].rearrange("p (j k) -> p j k", j=2)[:, :, P:T], ident_b[:, :], mask_b[:, 0:2, :],
                                         start=True, stop=False, skip_group_check=True)
                        for j in range(2):
                            done = nc.tensor.matmul(ps_m[:, u % 2, j * T:(j + 1) * T], QK[:, n, 2 * jp + j, g, P:T], QK[:, n, NJ, g, :],
                                                    start=False, stop=(j == 1), skip_group_check=True)
                    done.then_inc(s_b, 1)

            def values(c, g):
                n = c.of(NB)
                need(pe, s_k, 12 * c + (3 * g + 3))
                need(pe, s_ot, 4 * c + g)
                for j in range(NJ):
                    h = 4 * g + j
                    nc.tensor.matmul(ps_o[32 * j:32 * j + VW, g % 2, :], V[:, n, 0, h, :],
                                     PT[:, g % 2, 1 + j // 2, (j % 2) * T:(j % 2 + 1) * T], start=True, stop=False, skip_group_check=True)
                for j in range(NJ):
                    h = 4 * g + j
                    last = nc.tensor.matmul(ps_o[32 * j:32 * j + VW, g % 2, P:T], V[:, n, 1, h, :],
                                            PT[:, g % 2, 0, j * P:(j + 1) * P], start=False, stop=True, skip_group_check=True)
                last.then_inc(s_pv, 1)

            def o_rows(c, g):
                need(pe, s_ot, 4 * c + (g + 1))
                for t in range(2):
                    last = nc.tensor.transpose(ps_x[:, OB[g], t * P:(t + 1) * P], OT[:, g % 2, t * P:(t + 1) * P], ident[:, :])
                last.then_inc(s_ott, 1)

            def step(s):
                a, b, b1, c, p = s - 1, s - 2, s - 3, s - 4, s - 5
                A, BB, B1, C, PP = a.exists(B), b.exists(B), b1.exists(B), c.exists(B), p.exists(B)
                if C:
                    scores(c, 0)
                if B1:
                    maxima(b1, 9, 11)
                if PP:
                    values(p, 3)
                if B1:
                    maxima(b1, 11, 12)
                if PP:
                    need(pe, s_r, p)
                    o_rows(p, 2)
                if BB:
                    maxima(b, 0, 1)
                if A:
                    need(pe, s_xn, a + 1)
                    need(pe, s_att, 4 * p + 2)
                    for t in range(2):
                        last = nc.tensor.transpose(ps_x[:, 1, t * P:(t + 1) * P], XN[:, a.of(NB), t, :], ident[:, :])
                    last.then_inc(s_xt, 1)
                if C:
                    scores(c, 1)
                if BB:
                    maxima(b, 1, 3)
                if B1:
                    need(pe, s_red, 12 * b1 + 12)
                    need(pe, s_att, 4 * p + 3)
                    for t in range(2):
                        last = nc.tensor.transpose(ps_x[0:HEADS, 0, t * P:(t + 1) * P], m_neg[:, b1.of(NB), t, :], ident[:, :])
                    last.then_inc(s_mt, 1)
                if C:
                    values(c, 0)
                if BB:
                    maxima(b, 3, 4)
                if A:
                    need(pe, s_xlo, a + 1)
                    for i in range(2):
                        w, out = slice(i * D, (i + 1) * D), ps_x[:, 1, i * T:(i + 1) * T]
                        nc.tensor.matmul(out, w_lo[:, w], xt_hi[:, :], start=True, stop=False)
                        nc.tensor.matmul(out, w_hi[:, w], xt_lo[:, :], start=False, stop=False)
                        last = nc.tensor.matmul(out, w_hi[:, w], xt_hi[:, :], start=False, stop=True)
                    last.then_inc(s_qk, 1)
                if PP:
                    need(pe, s_mtc, (b1 + 1).most(B))
                    need(pe, s_att, 4 * p + 3)
                    o_rows(p, 3)
                if BB:
                    maxima(b, 4, 5)
                if C:
                    scores(c, 2)
                    need(pe, s_qklo, (a + 1).most(B))
                    need(pe, s_att, 4 * p + 2)
                    o_rows(c, 0)
                if BB:
                    maxima(b, 5, 6)
                if C:
                    values(c, 1)
                if PP:
                    need(pe, s_att, 4 * p + 4)
                    for t in range(2):
                        last = nc.tensor.transpose(ps_x[:, 0, t * P:(t + 1) * P],
                                                   attn[:, p.of(NB), t].rearrange("p g j r -> p (g j r)"), ident[:, :])
                    last.then_inc(s_aT, 1)
                if BB:
                    maxima(b, 6, 7)
                if A:
                    need(pe, s_qklo, a + 1)
                    need(pe, s_att, 4 * c + 1)
                    for t in range(2):
                        x, out = slice(t * P, (t + 1) * P), ps_x[:, 1, t * P:(t + 1) * P]
                        nc.tensor.matmul(out, xt_hi[:, x], w_lo[:, 2 * D:], start=True, stop=False)
                        nc.tensor.matmul(out, xt_lo[:, x], w_hi[:, 2 * D:], start=False, stop=False)
                        last = nc.tensor.matmul(out, xt_hi[:, x], w_hi[:, 2 * D:], start=False, stop=True)
                    last.then_inc(s_v, 1)
                if C:
                    scores(c, 3)
                if BB:
                    maxima(b, 7, 8)
                if C:
                    values(c, 2)
                if PP:
                    need(pe, s_at, p + 1)
                    for t in range(2):
                        last = nc.tensor.matmul(ps_x[:, 0, t * P:(t + 1) * P], at[:, t * P:(t + 1) * P], wo[:, :], start=True, stop=True)
                    last.then_inc(s_wo, 1)
                if BB:
                    maxima(b, 8, 9)
                if C:
                    need(pe, s_vc, (a + 1).most(B))
                    need(pe, s_att, 4 * c + 1)
                    o_rows(c, 1)

            steps(pe, B, 5, NB, step, 12)


E, F = 8, 512
NF = F // P


def experts(nc, dram, const):
    GROUPS = NTILE // 4
    x1_t = dram["x1"].rearrange("(t p) d -> p t d", p=P)
    h_t = dram["h"].rearrange("(t p) d -> p t d", p=P)
    out_t = dram["out"].rearrange("b (h p) d -> p (b h) d", p=P)
    ident = const["ident"]
    ctx = ExitStack()
    with ctx:
        def sb(name, shape, dt=fp32):
            return ctx.enter_context(nc.sbuf_tensor(name, shape, dt))

        def sem(name):
            return ctx.enter_context(nc.semaphore(name))

        w1_f = sb("c_w1_f", [P, F])
        w1_hi = sb("c_w1_hi", [P, E, F], f32r)
        w1_lo = sb("c_w1_lo", [P, E, F], f32r)
        w2 = sb("c_w2", [P, E, NF, D])
        wg_f = sb("c_wg_f", [P, E])
        bb1 = sb("c_bb1", [P, E, NF])
        bb2 = sb("c_bb2", [E, D])
        g_b = sb("c_g", [P, 1, D])
        b_b = sb("c_b", [P, 1, D])
        eps_ln = sb("c_eps", [P, 1])
        iota = sb("c_iota", [P, E])
        X = sb("c_X", [P, 2, 4, D])
        H = sb("c_H", [P, 2, 4, D])
        ht = sb("c_ht", [P, 2, 512])
        ht_hi = sb("c_ht_hi", [P, 2, 512], f32r)
        ht_lo = sb("c_ht_lo", [P, 2, 512], f32r)
        logits = sb("c_logits", [P, 4, E])
        top = sb("c_top", [P, 4, E])
        idx = sb("c_idx", [P, 4, E], u32)
        idx_f = sb("c_idx_f", [P, 4, 2])
        gap = sb("c_gap", [P, 4])
        e1 = sb("c_e1", [P, 4])
        den = sb("c_den", [P, 4])
        wt = sb("c_wt", [P, 4, 2])
        wa = sb("c_wa", [P, 4, E])
        w = sb("c_w", [P, 2, 4, E])
        wT = sb("c_wT", [E, 512])
        h1 = sb("c_h1", [P, 4, 512])
        acc = sb("c_acc", [P, 2, 4, D])
        stats = sb("c_stats", [P, 4, 6])
        mv = sb("c_mv", [P, 4, 2])
        lnv = sb("c_lnv", [P, 4])
        rstd = sb("c_rstd", [P, 4])
        Y0 = sb("c_Y0", [P, 4, D])
        Y1 = sb("c_Y1", [P, 4, D])
        Y2 = sb("c_Y2", [P, 4, D])
        Y3 = sb("c_Y3", [P, 2, 4, D])
        ps_t = ctx.enter_context(nc.psum_tensor("c_ps_t", [P, 512], fp32))
        ps_l = ctx.enter_context(nc.psum_tensor("c_ps_l", [P, 512], fp32))
        ps_1 = ctx.enter_context(nc.psum_tensor("c_ps_1", [P, 4, 512], fp32))
        ps_2 = ctx.enter_context(nc.psum_tensor("c_ps_2", [P, 2, 512], fp32))

        names = ("load w1f w1hi w1lo eps iota t ht hthi htlo l lg top idx idxf gap e1 den w0 w1 wa w wT wTc a h1 y acc b2 accb st mv "
                 "lnv rstd y0 y1 y2 y3").split()
        S = {n: sem("c_" + n) for n in names}
        s_in = [sem(f"c_in{k}") for k in range(2)]
        s_out = [sem(f"c_out{k}") for k in range(2)]
        block = ctx.enter_context(nc.Block())

        @block.sync
        def _(sync):
            sync.dma_start(wg_f[:, :], dram["wg"]).then_inc(S["load"], 16)
            sync.dma_start(w2[:, :, :, :], dram["w2"].rearrange("e (c p) d -> p e c d", p=P)).then_inc(S["load"], 16)
            sync.dma_start(bb1[:, :, :], dram["bb1"].rearrange("e (c p) -> p e c", p=P), allow_slow_non_contiguous=True).then_inc(S["load"], 16)
            sync.dma_start(bb2[:, :], dram["bb2"]).then_inc(S["load"], 16)
            sync.dma_start(g_b[:, 0, :], dram["g2"].partition_broadcast(P)).then_inc(S["load"], 16)
            sync.dma_start(b_b[:, 0, :], dram["b2"].partition_broadcast(P)).then_inc(S["load"], 16)
            for e in range(E):
                if e:
                    sync.wait_ge(S["w1lo"], e)
                sync.dma_start(w1_f[:, :], dram["w1"][e]).then_inc(S["w1f"], 16)

            sync.wait_ge(S["load"], 96)

            def step(s):
                if s.exists(GROUPS):
                    n = s.of(2)
                    need_apart(sync, (S["load"], 96), (S["y3"], s - 1))
                    sync.dma_start(H[:, n], h_t[:, bass.ds((s * 4).value(), 4), :]).then_inc(s_in[n], 16)
                    sync.dma_start(X[:, n], x1_t[:, bass.ds((s * 4).value(), 4), :]).then_inc(s_in[n], 16)
                if (s - 1).exists(GROUPS):
                    g = s - 1
                    need_apart(sync, (S["load"], 96), (S["y3"], g + 1))
                    sync.dma_start(out_t[:, bass.ds((g * 4).value(), 4), :], Y3[:, g.of(2)]).then_inc(s_out[g.of(2)], 16)

            steps(sync, GROUPS, 1, 2, step, 4)
            for k in range(2):
                sync.wait_ge(s_out[k], 16 * GROUPS // 2)

        @block.gpsimd
        def _(pool):
            nc.gpsimd.iota(iota[:, :], pattern=[[1, E]], base=0, channel_multiplier=0, allow_small_or_imprecise_dtypes=True).then_inc(S["iota"], 1)
            pool.wait_ge(S["load"], 96)

            def step(s):
                g, n = s, s.of(2)
                need(pool, S["y0"], g + 1)
                need(pool, S["y2"], g)
                nc.gpsimd.tensor_tensor(Y1[:, :, :], Y0[:, :, :], g_b[:, :, :].to_broadcast([P, 4, D]), ALU.mult).then_inc(S["y1"], 1)
                need(pool, S["y1"], g + 1)
                nc.gpsimd.tensor_tensor(Y2[:, :, :], Y1[:, :, :], b_b[:, :, :].to_broadcast([P, 4, D]), ALU.add).then_inc(S["y2"], 1)
                need(pool, S["y2"], g + 1)
                need(pool, s_out[n], g.turn(2) * 16)
                nc.gpsimd.tensor_tensor(Y3[:, n], Y2[:, :, :], X[:, n], ALU.add).then_inc(S["y3"], 1)

            steps(pool, GROUPS, 0, 2, step, 2)

        @block.scalar
        def _(act):
            for e in range(E):
                act.wait_ge(S["w1f"], 16 * e + 16)
                nc.scalar.copy(w1_hi[:, e, :], w1_f[:, :]).then_inc(S["w1hi"], 1)
            act.wait_ge(S["load"], 96)
            act.wait_ge(S["eps"], 1)

            def step(s):
                g, n = s, s.of(2)
                need(act, S["t"], g + 1)
                nc.scalar.copy(ht_hi[:, n], ps_t[:, :]).then_inc(S["hthi"], 1)
                nc.scalar.copy(ht[:, n], ps_t[:, :]).then_inc(S["ht"], 1)
                need(act, S["gap"], g + 1)
                nc.scalar.activation(e1[:, :], gap[:, :], ACT.Exp).then_inc(S["e1"], 1)
                need(act, S["wT"], g + 1)
                nc.scalar.copy(wT[:, :], ps_l[0:E, :]).then_inc(S["wTc"], 1)
                for e in range(E):
                    for c in range(NF):
                        q = 4 * e + c
                        need(act, S["a"], 32 * g + (q + 1))
                        need(act, S["y"], 32 * g + (q - 3))
                        nc.scalar.activation(h1[:, c], ps_1[:, c], ACT.Gelu_apprx_tanh, bias=bb1[:, e, c:c + 1]).then_inc(S["h1"], 1)
                need(act, S["mv"], g + 1)
                nc.scalar.activation(lnv[:, :], mv[:, :, 1], ACT.Ln, bias=eps_ln[:, :]).then_inc(S["lnv"], 1)
                need(act, S["lnv"], g + 1)
                nc.scalar.activation(rstd[:, :], lnv[:, :], ACT.Exp, scale=-0.5).then_inc(S["rstd"], 1)

            steps(act, GROUPS, 0, 2, step, 2)

        @block.vector
        def _(dve):
            nc.vector.memset(eps_ln[:, :], LN_EPS).then_inc(S["eps"], 1)
            for e in range(E):
                dve.wait_ge(S["w1hi"], e + 1)
                nc.vector.tensor_tensor(w1_lo[:, e, :], w1_f[:, :], w1_hi[:, e, :].bitcast(fp32), ALU.subtract).then_inc(S["w1lo"], 1)
            dve.wait_ge(S["iota"], 1)

            def step(s):
                g, n = s, s.of(2)
                need(dve, S["hthi"], g + 1)
                need(dve, S["ht"], g + 1)
                nc.vector.tensor_tensor(ht_lo[:, n], ps_t[:, :], ht_hi[:, n].bitcast(fp32), ALU.subtract).then_inc(S["htlo"], 1)
                need(dve, S["l"], g + 1)
                nc.vector.tensor_copy(logits[:, :, :], ps_l[:, 0:4 * E].rearrange("p (t e) -> p t e", e=E)).then_inc(S["lg"], 1)
                need_apart(dve, (S["iota"], 1), (S["lg"], g + 1))
                for t in range(4):
                    last = nc.vector.max(top[:, t, :], logits[:, t, :])
                last.then_inc(S["top"], 1)
                need_apart(dve, (S["iota"], 1), (S["top"], g + 1))
                for t in range(4):
                    last = nc.vector.max_index(idx[:, t, :], top[:, t, :], logits[:, t, :])
                last.then_inc(S["idx"], 1)
                nc.vector.tensor_tensor(gap[:, :], top[:, :, 1], top[:, :, 0], ALU.subtract).then_inc(S["gap"], 1)
                need(dve, S["idx"], g + 1)
                nc.vector.tensor_copy(idx_f[:, :, :], idx[:, :, 0:2]).then_inc(S["idxf"], 1)
                need(dve, S["e1"], g + 1)
                nc.vector.tensor_scalar(den[:, :], e1[:, :], 1.0, None, ALU.add).then_inc(S["den"], 1)
                need(dve, S["den"], g + 1)
                nc.vector.reciprocal(wt[:, :, 0], den[:, :]).then_inc(S["w0"], 1)
                need(dve, S["w0"], g + 1)
                nc.vector.tensor_tensor(wt[:, :, 1], wt[:, :, 0], e1[:, :], ALU.mult).then_inc(S["w1"], 1)
                need(dve, S["w1"], g + 1)
                need(dve, S["idxf"], g + 1)
                for t in range(4):
                    last = nc.vector.tensor_scalar(wa[:, t, :], iota[:, :], idx_f[:, t, 0:1], wt[:, t, 0:1], ALU.is_equal, ALU.mult)
                last.then_inc(S["wa"], 1)
                for t in range(4):
                    last = nc.vector.tensor_scalar(logits[:, t, :], iota[:, :], idx_f[:, t, 1:2], wt[:, t, 1:2], ALU.is_equal, ALU.mult)
                last.then_inc(S["wa"], 1)
                need(dve, S["wa"], 2 * g + 2)
                nc.vector.tensor_tensor(w[:, n], wa[:, :, :], logits[:, :, :], ALU.add).then_inc(S["w"], 1)
                need(dve, S["b2"], g + 1)
                nc.vector.tensor_tensor(acc[:, 1], ps_l[:, :].rearrange("p (t d) -> p t d", t=4), H[:, n], ALU.add).then_inc(S["accb"], 1)
                need(dve, S["w"], g + 1)
                need(dve, S["accb"], g + 1)
                for e in range(E):
                    need(dve, S["y"], 32 * g + (4 * e + 4))
                    need(dve, S["acc"], 8 * g + e)
                    for t in range(4):
                        last = nc.vector.scalar_tensor_tensor(out=acc[:, e % 2, t, :], in0=ps_2[:, e % 2, t * P:(t + 1) * P],
                                                              scalar=w[:, n, t, e:e + 1], in1=acc[:, (e + 1) % 2, t, :],
                                                              op0=ALU.mult, op1=ALU.add)
                    last.then_inc(S["acc"], 1)
                need(dve, S["acc"], 8 * g + 8)
                for t in range(4):
                    last = nc.vector.bn_stats(stats[:, t, :], acc[:, 1, t, :])
                last.then_inc(S["st"], 1)
                need_apart(dve, (S["iota"], 1), (S["st"], g + 1))
                for t in range(4):
                    last = nc.vector.bn_aggr(mv[:, t, :], stats[:, t, :])
                last.then_inc(S["mv"], 1)
                need(dve, S["rstd"], g + 1)
                need(dve, S["y1"], g)
                for t in range(4):
                    last = nc.vector.tensor_scalar(Y0[:, t, :], acc[:, 1, t, :], mv[:, t, 0:1], rstd[:, t:t + 1], ALU.subtract, ALU.mult)
                last.then_inc(S["y0"], 1)

            steps(dve, GROUPS, 0, 2, step, 2)

        @block.tensor
        def _(pe):
            pe.wait_ge(S["w1lo"], E)
            pe.wait_ge(S["load"], 96)

            def step(s):
                g, n = s, s.of(2)
                need(pe, s_in[n], g.turn(2) * 32 + 32)
                need(pe, S["htlo"], g)
                need(pe, S["ht"], g)
                for t in range(4):
                    last = nc.tensor.transpose(ps_t[:, t * P:(t + 1) * P], H[:, n, t, :], ident[:, :])
                last.then_inc(S["t"], 1)
                need(pe, S["ht"], g + 1)
                need(pe, S["accb"], g)
                for t in range(4):
                    last = nc.tensor.matmul(ps_l[:, t * E:(t + 1) * E], ht[:, n, t * P:(t + 1) * P], wg_f[:, :], start=True, stop=True)
                last.then_inc(S["l"], 1)
                need(pe, S["w"], g + 1)
                for t in range(4):
                    last = nc.tensor.transpose(ps_l[0:E, t * P:(t + 1) * P], w[:, n, t, :], ident[:, :])
                last.then_inc(S["wT"], 1)
                need(pe, S["wTc"], g + 1)
                for t in range(4):
                    last = nc.tensor.matmul(ps_l[:, t * P:(t + 1) * P], wT[:, t * P:(t + 1) * P], bb2[:, :], start=True, stop=True)
                last.then_inc(S["b2"], 1)
                need(pe, S["htlo"], g + 1)

                def down(e):
                    need(pe, S["acc"], 8 * g + (e - 1))
                    for c in range(NF):
                        need(pe, S["h1"], 32 * g + (4 * e + c + 1))
                        for t in range(4):
                            last = nc.tensor.matmul(ps_2[:, e % 2, t * P:(t + 1) * P], h1[:, c, t * P:(t + 1) * P], w2[:, e, c, :],
                                                    start=(c == 0 and t == 0), stop=(c == NF - 1), skip_group_check=True)
                        last.then_inc(S["y"], 1)

                for e in range(E):
                    for c in range(NF):
                        q = 4 * e + c
                        need(pe, S["h1"], 32 * g + (q - 3))
                        wc = slice(c * P, (c + 1) * P)
                        nc.tensor.matmul(ps_1[:, c], w1_lo[:, e, wc], ht_hi[:, n], start=True, stop=False)
                        nc.tensor.matmul(ps_1[:, c], w1_hi[:, e, wc], ht_lo[:, n], start=False, stop=False)
                        nc.tensor.matmul(ps_1[:, c], w1_hi[:, e, wc], ht_hi[:, n], start=False, stop=True).then_inc(S["a"], 1)
                    if e:
                        down(e - 1)
                down(E - 1)

            steps(pe, GROUPS, 0, 2, step, 2)


def constants(nc, ctx):
    ident = ctx.enter_context(nc.sbuf_tensor("ident", [P, P], fp32))
    ident_b = ctx.enter_context(nc.sbuf_tensor("ident_b", [P, P], bf16))
    mask_b = ctx.enter_context(nc.sbuf_tensor("mask_b", [P, 4, P], bf16))
    s_zero = ctx.enter_context(nc.semaphore("s_zero"))
    with nc.Block() as block:

        @block.gpsimd
        def _(pool):
            nc.gpsimd.memset(ident[:, :], 0.0)
            nc.gpsimd.memset(ident_b[:, :], 0.0)
            nc.gpsimd.memset(mask_b[:, :, :], 0.0).then_inc(s_zero, 1)
            pool.wait_ge(s_zero, 1)
            for m in (ident, ident_b):
                nc.gpsimd.affine_select(out=m[:, :], in_=m[:, :], compare_op=ALU.not_equal, fill=1.0, base=0,
                                        pattern=[[-1, P]], channel_multiplier=1)
            nc.gpsimd.affine_select(out=mask_b[:, :, :], in_=mask_b[:, :, :], compare_op=ALU.is_ge, fill=NEG, base=0,
                                    pattern=[[0, 4], [-1, P]], channel_multiplier=1).then_inc(s_zero, 1)
            pool.wait_ge(s_zero, 2)

    return dict(ident=ident, ident_b=ident_b, mask_b=mask_b)


def build(nc, dram):
    dram["x1"] = nc.dram_tensor("x1", (B * T, D), fp32).ap()
    dram["h"] = nc.dram_tensor("h", (B * T, D), fp32).ap()
    dram["qk_scr"] = nc.dram_tensor("qk_scr", (NB, 2 * PARTS, P, T), fp32).ap()
    with ExitStack() as ctx:
        const = constants(nc, ctx)
        recurrent_layer(nc, dram, const)
        attention(nc, dram, const)
        experts(nc, dram, const)


_INS = {
    "L0_attn_x": "x", "L0_attn_W": "W", "L0_attn_b": "b", "L0_attn_input_bias": "input_bias", "L0_attn_scale": "scale",
    "L0_ffn_w_qkv": "w_qkv", "L0_ffn_w_o": "w_o", "L0_ffn_g1": "g1", "L0_ffn_b1": "b1", "L0_ffn_wg": "wg",
    "L0_ffn_w1": "w1", "L0_ffn_bb1": "bb1", "L0_ffn_w2": "w2", "L0_ffn_bb2": "bb2", "L0_ffn_g2": "g2", "L0_ffn_b2": "b2",
}


def kernel(**inputs):
    import numpy as _np
    import concourse.bacc as _bacc
    from concourse.bass_utils import run_bass_kernel_spmd as _run

    nc = _bacc.Bacc("TRN2", target_bir_lowering=False, num_devices=1)
    arrays, dram = {}, {}
    for name, short in _INS.items():
        a = _np.ascontiguousarray(inputs[name])
        arrays[f"in_{name}_dram"] = a
        dram[short] = nc.dram_tensor(f"in_{name}_dram", a.shape, mybir.dt.from_np(a.dtype), kind="ExternalInput").ap()
    dram["out"] = nc.dram_tensor("out_0_dram", (B, T, D), fp32, kind="ExternalOutput").ap()
    build(nc, dram)
    r = _run(nc, [arrays], core_ids=[0])
    return r.results[0]["out_0_dram"]
```
